# Optimizing a Trainium2 kernel written in Bass

```python
import numpy as np
import jax
import jax.numpy as jnp

def _softmax(x, axis=-1):
    return jax.nn.softmax(x, axis=axis)

def _gelu(x):
    return jax.nn.gelu(x, approximate=True)

def _silu(x):
    return jax.nn.silu(x)

def _sigmoid(x):
    return jax.nn.sigmoid(x)

def _layernorm(x, axis=-1, eps=1e-05):
    m = jnp.mean(x, axis=axis, keepdims=True)
    v = jnp.var(x, axis=axis, keepdims=True)
    return (x - m) / jnp.sqrt(v + eps)

def _scatter_add(tgt, idx, src, axis=0):
    return tgt.at[idx].add(src)

def _segment_sum(src, seg, n):
    return jax.ops.segment_sum(src, seg, n)
kernel_name = 'mk_seq_postln_d2_jaxref_r8_1ad02a'

def setup_inputs(seed: int=0):
    np.random.seed(seed)
    _w = jnp.asarray

    def _L0_attn_setup():
        import jax, jax.numpy as jnp
        import numpy as np
        B, N, D, H = (2, 256, 256, 16)
        HD = D // H
        CHUNK = 64
        BASE = 10000.0

        def _l2norm(x, eps=1e-06):
            return x * jax.lax.rsqrt(jnp.sum(x * x, axis=-1, keepdims=True) + eps)

        def _rope(x):
            n, d = (x.shape[1], x.shape[-1])
            inv = 1.0 / BASE ** (jnp.arange(0, d, 2, dtype=jnp.float32) / d)
            th = jnp.arange(n, dtype=jnp.float32)[:, None] * inv
            cos = jnp.cos(th)[None, :, None, :]
            sin = jnp.sin(th)[None, :, None, :]
            x1, x2 = jnp.split(x, 2, axis=-1)
            return jnp.concatenate([x1 * cos - x2 * sin, x1 * sin + x2 * cos], axis=-1)

        def _kernel_regression(k, v, beta):
            b, n, h, dk = k.shape
            dv = v.shape[-1]
            nc = n // CHUNK
            Kc = k.reshape(b, nc, CHUNK, h, dk).transpose(1, 0, 3, 2, 4)
            Vc = v.reshape(b, nc, CHUNK, h, dv).transpose(1, 0, 3, 2, 4)
            Bc = beta.reshape(b, nc, CHUNK, h).transpose(1, 0, 3, 2)
            eye = jnp.eye(CHUNK, dtype=k.dtype)

            def step(S, inp):
                K, V, bt = inp
                A = jnp.tril(jnp.einsum('bhik,bhjk->bhij', K, K) * bt[:, :, None, :], -1)
                rhs = V - jnp.einsum('bhck,bhkv->bhcv', K, S)
                Vn = jax.scipy.linalg.solve_triangular(eye + A, rhs, lower=True)
                S = S + jnp.einsum('bhck,bhcv->bhkv', K * bt[..., None], Vn)
                return (S, Vn)
            S0 = jnp.zeros((b, h, dk, dv), k.dtype)
            S, Vn = jax.lax.scan(step, S0, (Kc, Vc, Bc))
            v_new = Vn.transpose(1, 0, 3, 2, 4).reshape(b, n, h, dv)
            return (v_new, S)
        key = jax.random.key(seed)
        ks = jax.random.split(key, 6)
        s = 0.02
        return {'x': jax.random.normal(ks[0], (B, N, D), jnp.float32), 'Wq': jax.random.normal(ks[1], (D, D), jnp.float32) * s, 'Wk': jax.random.normal(ks[2], (D, D), jnp.float32) * s, 'Wv': jax.random.normal(ks[3], (D, D), jnp.float32) * s, 'Wo': jax.random.normal(ks[4], (D, D), jnp.float32) * s, 'Wb': jax.random.normal(ks[5], (D, H), jnp.float32) * s}
    _L0_attn_in = _L0_attn_setup()

    def _L0_ffn_setup():
        import jax, jax.numpy as jnp
        import numpy as np
        import math
        B, S, D = (2, 256, 256)
        P = 4
        PW = 2
        L = 2
        STD = 0.02
        EPS = 1e-05

        def _layer_norm(x, g, b):
            m = jnp.mean(x, axis=-1, keepdims=True)
            v = jnp.mean(jnp.square(x - m), axis=-1, keepdims=True)
            return (x - m) * jax.lax.rsqrt(v + EPS) * g + b
        key = jax.random.key(seed)
        ks = jax.random.split(key, 16)
        n = lambda k, shape: jax.random.normal(k, shape, dtype=jnp.float32) * STD
        inp = {'x': jax.random.normal(ks[0], (B, S, D), dtype=jnp.float32), 'amp_w': n(ks[1], (D, D)), 'amp_b': jnp.zeros((D,), jnp.float32), 'ph_w': n(ks[2], (D, D)), 'ph_b': jnp.zeros((D,), jnp.float32), 'ent_w': n(ks[3], (L, D, P * D)), 'ent_b': jnp.zeros((L, P * D), jnp.float32), 'ent_pw': n(ks[4], (L, P * D, D)), 'ent_pb': jnp.zeros((L, D), jnp.float32), 'path_w': n(ks[5], (L, PW, D, D)), 'path_b': jnp.zeros((L, PW, D), jnp.float32), 'phase': jax.random.normal(ks[6], (L, PW, D), dtype=jnp.float32), 'ln3_g': jnp.ones((L, D), jnp.float32), 'ln3_b': jnp.zeros((L, D), jnp.float32), 'ln4_g': jnp.ones((L, D), jnp.float32), 'ln4_b': jnp.zeros((L, D), jnp.float32)}
        return inp
    _L0_ffn_in = _L0_ffn_setup()

    def _L1_attn_setup():
        import jax, jax.numpy as jnp
        import numpy as np
        NUM_HEADS = 16
        key = jax.random.key(seed)
        k0, k1, k2 = jax.random.split(key, 3)
        B, S, D = (2, 256, 256)
        hd = D // NUM_HEADS
        hidden_states = jax.random.normal(k0, (B, S, D), dtype=jnp.float32)
        c_attn_w = jax.random.normal(k1, (D + 2 * hd, D), dtype=jnp.float32) * 0.02
        c_attn_b = jnp.zeros((D + 2 * hd,), dtype=jnp.float32)
        c_proj_w = jax.random.normal(k2, (D, D), dtype=jnp.float32) * 0.02
        c_proj_b = jnp.zeros((D,), dtype=jnp.float32)
        return {'hidden_states': hidden_states, 'c_attn_w': c_attn_w, 'c_attn_b': c_attn_b, 'c_proj_w': c_proj_w, 'c_proj_b': c_proj_b}
    _L1_attn_in = _L1_attn_setup()

    def _L1_ffn_setup():
        import jax, jax.numpy as jnp
        import numpy as np
        B, S, H, E = (4, 256, 256, 8)
        key = jax.random.key(seed)
        k1, k2, k3 = jax.random.split(key, 3)
        x = jax.random.normal(k1, (B, S, H), dtype=jnp.float32)
        Wg = jax.random.normal(k2, (H, E), dtype=jnp.float32) * 0.02
        W = jax.random.normal(k3, (E, H, H), dtype=jnp.float32) * 0.02
        b = jnp.zeros((E, H), dtype=jnp.float32)
        return {'x': x, 'Wg': Wg, 'W': W, 'b': b}
    _L1_ffn_in = _L1_ffn_setup()
    _d = {'L0_attn_x': _L0_attn_in['x'], 'L0_attn_Wq': _L0_attn_in['Wq'], 'L0_attn_Wk': _L0_attn_in['Wk'], 'L0_attn_Wv': _L0_attn_in['Wv'], 'L0_attn_Wo': _L0_attn_in['Wo'], 'L0_attn_Wb': _L0_attn_in['Wb'], 'L0_ffn_amp_w': _L0_ffn_in['amp_w'], 'L0_ffn_amp_b': _L0_ffn_in['amp_b'], 'L0_ffn_ph_w': _L0_ffn_in['ph_w'], 'L0_ffn_ph_b': _L0_ffn_in['ph_b'], 'L0_ffn_ent_w': _L0_ffn_in['ent_w'], 'L0_ffn_ent_b': _L0_ffn_in['ent_b'], 'L0_ffn_ent_pw': _L0_ffn_in['ent_pw'], 'L0_ffn_ent_pb': _L0_ffn_in['ent_pb'], 'L0_ffn_path_w': _L0_ffn_in['path_w'], 'L0_ffn_path_b': _L0_ffn_in['path_b'], 'L0_ffn_phase': _L0_ffn_in['phase'], 'L0_ffn_ln3_g': _L0_ffn_in['ln3_g'], 'L0_ffn_ln3_b': _L0_ffn_in['ln3_b'], 'L0_ffn_ln4_g': _L0_ffn_in['ln4_g'], 'L0_ffn_ln4_b': _L0_ffn_in['ln4_b'], 'L1_attn_c_attn_w': _L1_attn_in['c_attn_w'], 'L1_attn_c_attn_b': _L1_attn_in['c_attn_b'], 'L1_attn_c_proj_w': _L1_attn_in['c_proj_w'], 'L1_attn_c_proj_b': _L1_attn_in['c_proj_b'], 'L1_ffn_Wg': _L1_ffn_in['Wg'], 'L1_ffn_W': _L1_ffn_in['W'], 'L1_ffn_b': _L1_ffn_in['b']}
    _x0 = _d['L0_attn_x']
    _d['L0_attn_x'] = jax.random.normal(jax.random.fold_in(jax.random.key(seed), 1), (4, 512, 256), dtype=_x0.dtype)
    del _x0
    return _d

def reference(L0_attn_x, L0_attn_Wq, L0_attn_Wk, L0_attn_Wv, L0_attn_Wo, L0_attn_Wb, L0_ffn_amp_w, L0_ffn_amp_b, L0_ffn_ph_w, L0_ffn_ph_b, L0_ffn_ent_w, L0_ffn_ent_b, L0_ffn_ent_pw, L0_ffn_ent_pb, L0_ffn_path_w, L0_ffn_path_b, L0_ffn_phase, L0_ffn_ln3_g, L0_ffn_ln3_b, L0_ffn_ln4_g, L0_ffn_ln4_b, L1_attn_c_attn_w, L1_attn_c_attn_b, L1_attn_c_proj_w, L1_attn_c_proj_b, L1_ffn_Wg, L1_ffn_W, L1_ffn_b):

    def _L0_attn_ref(x, Wq, Wk, Wv, Wo, Wb):
        import jax, jax.numpy as jnp
        import numpy as np
        B, N, D, H = (2, 256, 256, 16)
        HD = D // H
        CHUNK = 64
        BASE = 10000.0

        def _l2norm(x, eps=1e-06):
            return x * jax.lax.rsqrt(jnp.sum(x * x, axis=-1, keepdims=True) + eps)

        def _rope(x):
            n, d = (x.shape[1], x.shape[-1])
            inv = 1.0 / BASE ** (jnp.arange(0, d, 2, dtype=jnp.float32) / d)
            th = jnp.arange(n, dtype=jnp.float32)[:, None] * inv
            cos = jnp.cos(th)[None, :, None, :]
            sin = jnp.sin(th)[None, :, None, :]
            x1, x2 = jnp.split(x, 2, axis=-1)
            return jnp.concatenate([x1 * cos - x2 * sin, x1 * sin + x2 * cos], axis=-1)

        def _kernel_regression(k, v, beta):
            b, n, h, dk = k.shape
            dv = v.shape[-1]
            nc = n // CHUNK
            Kc = k.reshape(b, nc, CHUNK, h, dk).transpose(1, 0, 3, 2, 4)
            Vc = v.reshape(b, nc, CHUNK, h, dv).transpose(1, 0, 3, 2, 4)
            Bc = beta.reshape(b, nc, CHUNK, h).transpose(1, 0, 3, 2)
            eye = jnp.eye(CHUNK, dtype=k.dtype)

            def step(S, inp):
                K, V, bt = inp
                A = jnp.tril(jnp.einsum('bhik,bhjk->bhij', K, K) * bt[:, :, None, :], -1)
                rhs = V - jnp.einsum('bhck,bhkv->bhcv', K, S)
                Vn = jax.scipy.linalg.solve_triangular(eye + A, rhs, lower=True)
                S = S + jnp.einsum('bhck,bhcv->bhkv', K * bt[..., None], Vn)
                return (S, Vn)
            S0 = jnp.zeros((b, h, dk, dv), k.dtype)
            S, Vn = jax.lax.scan(step, S0, (Kc, Vc, Bc))
            v_new = Vn.transpose(1, 0, 3, 2, 4).reshape(b, n, h, dv)
            return (v_new, S)
        b, n, d = x.shape
        q = (x @ Wq).reshape(b, n, H, HD)
        k = _l2norm((x @ Wk).reshape(b, n, H, HD))
        v = (x @ Wv).reshape(b, n, H, HD)
        beta = 2.0 * jax.nn.sigmoid(x @ Wb)
        q = _rope(q)
        k = _rope(k)
        v, _state = _kernel_regression(k, v, beta)
        k = k * beta[..., None]
        scale = HD ** (-0.5)
        scores = jnp.einsum('bqhd,bkhd->bhqk', q, k) * scale
        mask = jnp.tril(jnp.ones((n, n), bool))
        scores = jnp.where(mask, scores, -jnp.inf)
        attn = jax.nn.softmax(scores, axis=-1)
        out = jnp.einsum('bhqk,bkhd->bqhd', attn, v).reshape(b, n, d)
        return out @ Wo

    def _L0_ffn_ref(x, amp_w, amp_b, ph_w, ph_b, ent_w, ent_b, ent_pw, ent_pb, path_w, path_b, phase, ln3_g, ln3_b, ln4_g, ln4_b):
        import jax, jax.numpy as jnp
        import numpy as np
        import math
        B, S, D = (2, 256, 256)
        P = 4
        PW = 2
        L = 2
        STD = 0.02
        EPS = 1e-05

        def _layer_norm(x, g, b):
            m = jnp.mean(x, axis=-1, keepdims=True)
            v = jnp.mean(jnp.square(x - m), axis=-1, keepdims=True)
            return (x - m) * jax.lax.rsqrt(v + EPS) * g + b
        amp = jax.nn.sigmoid(x @ amp_w + amp_b)
        ph = jnp.tanh(x @ ph_w + ph_b) * math.pi
        h = (jnp.cos(ph) + jnp.sin(ph)) * amp
        for l in range(L):
            e = h @ ent_w[l] + ent_b[l]
            ent = e @ ent_pw[l] + ent_pb[l]
            h = _layer_norm(h + ent, ln3_g[l], ln3_b[l])
            t = jnp.einsum('bsd,pdf->pbsf', h, path_w[l]) + path_b[l][:, None, None, :]
            mod = jnp.cos(phase[l]) + jnp.sin(phase[l])
            interf = jnp.sum(t * mod[:, None, None, :], axis=0)
            h = _layer_norm(h + interf, ln4_g[l], ln4_b[l])
        return h

    def _L1_attn_ref(hidden_states, c_attn_w, c_attn_b, c_proj_w, c_proj_b):
        import jax, jax.numpy as jnp
        import numpy as np
        NUM_HEADS = 16
        B, S, D = hidden_states.shape
        H = NUM_HEADS
        hd = D // H
        scale = hd ** (-0.5)
        qkv = hidden_states @ c_attn_w.T + c_attn_b
        q = qkv[..., :D].reshape(B, S, H, hd)
        k = qkv[..., D:D + hd]
        v = qkv[..., D + hd:]
        scores = jnp.einsum('bqhd,bkd->bhqk', q, k) * scale
        causal = jnp.tril(jnp.ones((S, S), dtype=bool))
        scores = jnp.where(causal, scores, jnp.finfo(scores.dtype).min)
        attn = jax.nn.softmax(scores, axis=-1)
        ctx = jnp.einsum('bhqk,bkd->bqhd', attn, v).reshape(B, S, D)
        out = ctx @ c_proj_w.T + c_proj_b
        return out

    def _L1_ffn_ref(x, Wg, W, b):
        import jax, jax.numpy as jnp
        import numpy as np
        B, S, H, E = (4, 256, 256, 8)
        logits = jnp.einsum('bsh,he->bse', x, Wg)
        probs = jax.nn.softmax(logits, axis=-1)
        idx = jnp.argmax(probs, axis=-1)
        onehot = jax.nn.one_hot(idx, E, dtype=x.dtype)
        combine = onehot * probs
        y = jnp.einsum('bsh,ehd->bsed', x, W) + b
        out = jnp.einsum('bsed,bse->bsd', y, combine)
        return out
    x = L0_attn_x
    x = _layernorm(x + _L0_attn_ref(x, L0_attn_Wq, L0_attn_Wk, L0_attn_Wv, L0_attn_Wo, L0_attn_Wb), axis=-1)
    x = _layernorm(x + _L0_ffn_ref(x, L0_ffn_amp_w, L0_ffn_amp_b, L0_ffn_ph_w, L0_ffn_ph_b, L0_ffn_ent_w, L0_ffn_ent_b, L0_ffn_ent_pw, L0_ffn_ent_pb, L0_ffn_path_w, L0_ffn_path_b, L0_ffn_phase, L0_ffn_ln3_g, L0_ffn_ln3_b, L0_ffn_ln4_g, L0_ffn_ln4_b), axis=-1)
    x = _layernorm(x + _L1_attn_ref(x, L1_attn_c_attn_w, L1_attn_c_attn_b, L1_attn_c_proj_w, L1_attn_c_proj_b), axis=-1)
    x = _layernorm(x + _L1_ffn_ref(x, L1_ffn_Wg, L1_ffn_W, L1_ffn_b), axis=-1)
    return x

_drawn_inputs = setup_inputs


def setup_inputs(seed=0):
    import zlib

    import numpy as np

    out = dict(_drawn_inputs(seed))
    spreads = {'L0_ffn_amp_b': (0.0, 0.1),
     'L0_ffn_ph_b': (0.0, 0.1),
     'L0_ffn_ent_b': (0.0, 0.1),
     'L0_ffn_ent_pb': (0.0, 0.1),
     'L0_ffn_path_b': (0.0, 0.1),
     'L0_ffn_ln3_g': (1.0, 0.2),
     'L0_ffn_ln3_b': (0.0, 0.1),
     'L0_ffn_ln4_g': (1.0, 0.2),
     'L0_ffn_ln4_b': (0.0, 0.1),
     'L1_attn_c_attn_b': (0.0, 0.1),
     'L1_attn_c_proj_b': (0.0, 0.1),
     'L1_ffn_b': (0.0, 0.406)}
    factors = {'L0_attn_Wq': 8.0,
     'L0_attn_Wk': 5.887,
     'L0_attn_Wv': 3.461,
     'L0_attn_Wo': 3.451,
     'L0_attn_Wb': 8.0}
    for name, (base, spread) in spreads.items():
        noise = np.random.default_rng([zlib.crc32(name.encode()), seed]).standard_normal(out[name].shape)
        drawn = base * np.exp(spread * noise) if base else spread * noise
        out[name] = jnp.asarray(drawn.astype(out[name].dtype))
    for name, factor in factors.items():
        out[name] = (out[name] * factor).astype(out[name].dtype)
    return out
```

```python
from contextlib import ExitStack

import numpy as np

import concourse.bass as bass
from concourse import mybir

ALU = mybir.AluOpType
ACT = mybir.ActivationFunctionType
AX = mybir.AxisListType
F32 = mybir.dt.float32
BF16 = mybir.dt.bfloat16

P = 128
B, N, D, H = 4, 512, 256, 16
HD = D // H
KD = D // P
R = 32
NT = N // R
G4 = 4
NG = NT // G4
HG = H // 4
CH = 16
EPS_L2, EPS_LN = 1e-6, 1e-5
SCALE = HD ** -0.5
NPART = 3
PAIRS = [(0, 0), (0, 1), (1, 0), (1, 1), (0, 2), (2, 0)]
KR = 16 * len(PAIRS)
KRM = KR + NPART
E = 8
PI = float(np.pi)


class Ctx:
    pass


def semaphores(nc, ctx, prefix):
    held = []
    ctx.callback(lambda: (nc.clear_and_free_semaphores(held), nc.all_engine_barrier()))

    def sem(name):
        held.append(nc.alloc_semaphore(prefix + name))
        return held[-1]

    return sem


def bcast(ap, dims):
    return bass.AP(tensor=ap.tensor, offset=ap.offset, ap=[list(ap.ap[0])] + [list(d) for d in dims])


def rows_bcast(dram, offset, n):
    return bass.AP(tensor=dram.tensor, offset=dram.offset + offset, ap=[[0, P], [1, n]])


def phase_qkv(nc, g):
    with ExitStack() as ctx:
        sb = lambda n, s, d=F32: ctx.enter_context(nc.sbuf_tensor(n, s, d))
        sem = semaphores(nc, ctx, "")
        WC = 3 * D + H
        w = sb("l0_wqkvb", [P, KD, WC])
        xT = sb("l0_xT", [P, G4, KD, P])
        qk = g.QKR
        kn = sb("l0_kn_rows", [P, G4, H, 32])
        t1 = sb("rope_t1", [P, G4, 2 * D])
        t2 = sb("rope_t2", [P, G4, 2 * D])
        rem = sb("split_rem", [P, 2, 4, P])
        masks = rem[:, 0, 0:2, :]
        part = [sb(f"qk_part{p}", [P, 4, B, N], BF16) for p in range(NPART)]
        cosT, sinT = sb("rope_cos", [P, NT, HD]), sb("rope_sin", [P, NT, HD])
        ksq = sb("k_squares", [P, G4, D])
        ss = sb("k_sumsq", [P, G4, H])
        mhalf = g.mhalf
        ld_x, ld_w, ld_c = sem("x_loaded"), sem("w_loaded"), sem("consts_loaded")
        xT_ps, xT_sb = sem("xT_in_psum"), sem("xT_in_sbuf")
        qk_ps, v_ps, qk_sb, v_sb = sem("qk_in_psum"), sem("v_in_psum"), sem("qk_in_sbuf"), sem("v_in_sbuf")
        bexp, beta_ok = sem("beta_exp"), sem("beta_steps")
        pad_ok, cos_ok, sin_ok, rot_ok = sem("kn_pad_zeroed"), sem("cos_product"), sem("sin_product"), sem("rotated")
        sq_ok, ss_ok, rs_ok, kn_ok, kb_ok = sem("k_squared"), sem("k_sums"), sem("k_rsqrt"), sem("kn_rows"), sem("kb_rows")
        kt_ps, qt_ps, kt_sb, p1_ok, r1_ok, p2_ok, p3_ok = (sem("knT_psum"), sem("qkT_psum"), sem("knT_sbuf"), sem("part1"),
                                                         sem("remainder1"), sem("part2"), sem("part3"))
        st, cbf = sem("parts_stored"), sem("bf16_consts")
        ps = g.ps
        x_d = g.x_in
        block = ctx.enter_context(nc.Block())

        @block.sync
        def _(sp):
            for b in range(B):
                sp.dma_start(g.X[R * b:R * b + R, :, :], x_d[b].rearrange("(c i) d -> i c d", i=R)).then_inc(ld_x, 16)
            sp.dma_start(g.idf[:, :], g.ident_d).then_inc(ld_c, 16)
            sp.dma_start(masks[:, 0, :], g.maskq_d).then_inc(ld_c, 16)
            sp.dma_start(masks[:, 1, :], g.maskk_d).then_inc(ld_c, 16)
            sp.dma_start(cosT[:, :, :], g.cos_d).then_inc(ld_c, 16)
            sp.dma_start(sinT[:, :, :], g.sin_d).then_inc(ld_c, 16)
            sp.wait_ge(p3_ok, NT)
            for p in range(NPART):
                sp.dma_start(g.parts_d[p].rearrange("x p n -> p x n"),
                             part[p][:, :, :, :].rearrange("p x b n -> p x (b n)")).then_inc(st, 16)
            sp.wait_ge(st, 16 * NPART)

        @block.scalar
        def _(act):
            for j, wd in enumerate((g.Wq, g.Wk, g.Wv)):
                act.dma_start(w[:, :, j * D:(j + 1) * D], wd.rearrange("(k p) n -> p k n", p=P)).then_inc(ld_w, 16)
            act.dma_start(w[:, :, 3 * D:], g.Wb.rearrange("(k p) n -> p k n", p=P)).then_inc(ld_w, 16)

            def transposed(c):
                act.wait_ge(xT_ps, c + 1)
                if c >= G4:
                    act.wait_ge(v_ps, c - G4 + 1)
                nc.scalar.copy(xT[:, c % G4, :, :], ps[:, c % 2, 0:KD * P].rearrange("p (k m) -> p k m", k=KD)).then_inc(xT_sb, 1)

            def rows(c):
                act.wait_ge(qk_ps, c + 1)
                nc.scalar.copy(qk[:, c, :], ps[:, 2 + c % 2, :]).then_inc(qk_sb, 1)

            def operands(c):
                act.wait_ge(kt_ps, c + 1)
                nc.scalar.copy(g.KT[:, :, :, c * R:(c + 1) * R],
                               ps[:, 6, :].rearrange("p (g b i) -> p g b i", g=HG, b=B)).then_inc(kt_sb, 1)
                act.wait_ge(qt_ps, c + 1)
                nc.scalar.copy(part[0][:, :, :, c * R:(c + 1) * R],
                               ps[:, 7, :].rearrange("p (x b i) -> p x b i", x=4, b=B)).then_inc(p1_ok, 1)

            for q in range(NG + 1):
                for j in range(G4):
                    if q < NG:
                        transposed(q * G4 + j)
                        rows(q * G4 + j)
                if q < NG:
                    act.wait_ge(v_sb, (q + 1) * G4)
                    gs = slice(q * G4, (q + 1) * G4)
                    nc.scalar.activation(g.beta[:, gs, :], g.beta[:, gs, :], ACT.Exp, scale=-1.0).then_inc(bexp, 1)
                if q >= 1:
                    for j in range(G4):
                        operands((q - 1) * G4 + j)

        @block.vector
        def _(dve):
            nc.vector.memset(mhalf[:, :], -0.5).then_inc(pad_ok, 1)
            nc.vector.memset(kn[:, :, :, :], 0.0).then_inc(pad_ok, 1)

            def evac(c):
                dve.wait_ge(v_ps, c + 1)
                nc.vector.tensor_copy(g.V[:, c, :], ps[:, 4 + c % 2, 0:D])
                nc.vector.tensor_copy(g.beta[:, c, :], ps[:, 4 + c % 2, D:D + H]).then_inc(v_sb, 1)

            def group(q):
                gs = slice(q * G4, (q + 1) * G4)
                be = g.beta[:, gs, :]
                dve.wait_ge(bexp, q + 1)
                nc.vector.tensor_scalar(be, be, 0.5, 0.5, ALU.mult, ALU.add).then_inc(beta_ok, 1)
                dve.wait_ge(qk_sb, (q + 1) * G4)
                if q == 0:
                    dve.wait_ge(ld_c, 80)
                else:
                    dve.wait_ge(rot_ok, q)
                t1v = t1[:, :, :].rearrange("p c (h e) -> p c h e", e=HD)
                qv = qk[:, gs, :].rearrange("p c (h e) -> p c h e", e=HD)
                cv = bcast(cosT[:, gs, :], [[HD, G4], [0, 2 * H], [1, HD]])
                nc.vector.tensor_tensor(t1v, qv, cv, ALU.mult).then_inc(cos_ok, 1)
                dve.wait_ge(beta_ok, 2 * q + 1)
                nc.vector.reciprocal(be, be).then_inc(beta_ok, 1)
                dve.wait_ge(sq_ok, q + 1)
                nc.vector.tensor_reduce(ss[:, :, :], ksq[:, :, :].rearrange("p c (h e) -> p c h e", e=HD), AX.X, ALU.add).then_inc(ss_ok, 1)
                dve.wait_ge(sin_ok, 2 * (q + 1))
                dve.wait_ge(cos_ok, q + 1)
                nc.vector.tensor_tensor(qk[:, gs, :], t1[:, :, :], t2[:, :, :], ALU.add).then_inc(rot_ok, 1)

            def remainder(c):
                dve.wait_ge(p1_ok, c + 1)
                if c == 0:
                    dve.wait_ge(cbf, 3)
                if c >= 2:
                    dve.wait_ge(p3_ok, c - 1)
                nc.vector.tensor_tensor(rem[:, c % 2, :, :].rearrange("p x (b i) -> p x b i", b=B),
                                        ps[:, 7, :].rearrange("p (x b i) -> p x b i", x=4, b=B),
                                        part[0][:, :, :, c * R:(c + 1) * R], ALU.subtract).then_inc(r1_ok, 1)

            for q in range(NG + 1):
                if q < NG:
                    for j in range(G4):
                        evac(q * G4 + j)
                if q >= 1:
                    for j in range(G4):
                        remainder((q - 1) * G4 + j)
                if q < NG:
                    group(q)

        @block.gpsimd
        def _(pool):
            def group(q):
                gs = slice(q * G4, (q + 1) * G4)
                qv = qk[:, gs, :].rearrange("p c (h e) -> p c h e", e=HD)
                t2v = t2[:, :, :].rearrange("p c (h e) -> p c h e", e=HD)
                pool.wait_ge(qk_sb, (q + 1) * G4)
                if q == 0:
                    pool.wait_ge(ld_c, 80)
                else:
                    pool.wait_ge(rot_ok, q)
                if q >= 1:
                    pool.wait_ge(ss_ok, q)
                nc.gpsimd.tensor_tensor(ksq[:, :, :], qk[:, gs, D:], qk[:, gs, D:], ALU.mult).then_inc(sq_ok, 1)
                for lo, hi in ((0, 8), (8, 0)):
                    sv = bcast(sinT[:, gs, lo:lo + 8], [[HD, G4], [0, 2 * H], [1, 8]])
                    nc.gpsimd.tensor_tensor(t2v[:, :, :, lo:lo + 8], qv[:, :, :, hi:hi + 8], sv, ALU.mult).then_inc(sin_ok, 1)
                pool.wait_ge(ss_ok, q + 1)
                nc.gpsimd.tensor_scalar(ss[:, :, :], ss[:, :, :], 1.0, EPS_L2, ALU.mult, ALU.add).then_inc(rs_ok, 1)
                pool.wait_ge(rs_ok, 2 * q + 1)
                pool.wait_ge(pad_ok, 2)
                nc.gpsimd.tensor_tensor(ss[:, :, :], ss[:, :, :], mhalf[:, :].rearrange("p (c h) -> p c h", c=G4), ALU.pow).then_inc(rs_ok, 1)
                pool.wait_ge(rs_ok, 2 * q + 2)
                pool.wait_ge(rot_ok, q + 1)
                if q >= 1:
                    pool.wait_ge(kt_ps, q * G4)
                kv = qk[:, gs, D:].rearrange("p c (h e) -> p c h e", e=HD)
                nc.gpsimd.tensor_tensor(kn[:, :, :, 0:HD], kv, bcast(ss[:, :, :], [[H, G4], [1, H], [0, HD]]), ALU.mult).then_inc(kn_ok, 1)
                pool.wait_ge(kn_ok, q + 1)
                pool.wait_ge(beta_ok, 2 * q + 2)
                nc.gpsimd.tensor_tensor(g.KB[:, gs, :].rearrange("p c (h e) -> p c h e", e=HD), kn[:, :, :, 0:HD],
                                        bcast(g.beta[:, gs, :], [[H, G4], [1, H], [0, HD]]), ALU.mult).then_inc(kb_ok, 1)

            pool.wait_ge(ld_c, 80)
            for dst, src in ((g.idb, g.idf[:, :]), (g.maskq, masks[:, 0, :]), (g.maskk, masks[:, 1, :])):
                nc.gpsimd.tensor_copy(dst[:, :], src).then_inc(cbf, 1)

            def split(c):
                pool.wait_ge(r1_ok, c + 1)
                r = rem[:, c % 2, :, :].rearrange("p x (b i) -> p x b i", b=B)
                cs = slice(c * R, (c + 1) * R)
                nc.gpsimd.tensor_copy(part[1][:, :, :, cs], r).then_inc(p2_ok, 1)
                pool.wait_ge(p2_ok, c + 1)
                nc.gpsimd.tensor_tensor(part[2][:, :, :, cs], r, part[1][:, :, :, cs], ALU.subtract).then_inc(p3_ok, 1)

            for q in range(NG + 1):
                if q >= 1:
                    for j in range(G4):
                        split((q - 1) * G4 + j)
                if q < NG:
                    group(q)

        @block.tensor
        def _(pe):
            pe.wait_ge(ld_x, 64)
            pe.wait_ge(ld_c, 80)

            def xpose(c):
                if c >= 2:
                    pe.wait_ge(xT_sb, c - 1)
                for k in range(KD):
                    last = nc.tensor.transpose(ps[:, c % 2, k * P:(k + 1) * P], g.X[:, c, k * P:(k + 1) * P], g.idf[:, :])
                last.then_inc(xT_ps, 1)

            def project(c):
                pe.wait_ge(xT_sb, c + 1)
                if c == 0:
                    pe.wait_ge(ld_w, 64)
                if c >= 2:
                    pe.wait_ge(qk_sb, c - 1)
                    pe.wait_ge(v_sb, c - 1)
                for k in range(KD):
                    last = nc.tensor.matmul(ps[:, 2 + c % 2, :], xT[:, c % G4, k, :], w[:, k, 0:2 * D], start=(k == 0), stop=(k == KD - 1))
                last.then_inc(qk_ps, 1)
                for k in range(KD):
                    last = nc.tensor.matmul(ps[:, 4 + c % 2, 0:D + H], xT[:, c % G4, k, :], w[:, k, 2 * D:], start=(k == 0), stop=(k == KD - 1))
                last.then_inc(v_ps, 1)

            def operands(c):
                q, j = c // G4, c % G4
                pe.wait_ge(kn_ok, q + 1)
                if c >= 1:
                    pe.wait_ge(kt_sb, c)
                for x in range(HG):
                    last = nc.tensor.transpose(ps[:, 6, x * P:(x + 1) * P], kn[:, j, 4 * x:4 * x + 4, :].rearrange("p h e -> p (h e)"), g.idf[:, :])
                last.then_inc(kt_ps, 1)
                pe.wait_ge(kb_ok, q + 1)
                pe.wait_ge(rot_ok, q + 1)
                if c >= 1:
                    pe.wait_ge(r1_ok, c)
                for x in range(KD):
                    nc.tensor.transpose(ps[:, 7, x * P:(x + 1) * P], qk[:, c, x * P:(x + 1) * P], g.idf[:, :])
                for x in range(KD):
                    last = nc.tensor.transpose(ps[:, 7, (2 + x) * P:(3 + x) * P], g.KB[:, c, x * P:(x + 1) * P], g.idf[:, :])
                last.then_inc(qt_ps, 1)

            xpose(0)
            for c in range(NT):
                if c + 1 < NT:
                    xpose(c + 1)
                project(c)
                if c % G4 == G4 - 1 and c >= G4:
                    for j in range(G4):
                        operands((c // G4 - 1) * G4 + j)
            for j in range(G4):
                operands((NG - 1) * G4 + j)


def phase_delta(nc, g):
    with ExitStack() as ctx:
        sem = semaphores(nc, ctx, "")
        ps = g.ps
        with ExitStack() as c1:
            sb = lambda n, s, d=F32: c1.enter_context(nc.sbuf_tensor(n, s, d))
            AT = g.AT
            TT = g.TT
            TN = sb("inv_first", [P, NT, CH, H])
            L = sb("chunk_A", [P, CH, CH, H])
            T = sb("chunk_inv", [P, CH, CH, H])
            TC = L
            tmp = sb("update", [P, 64 * CH])
            Xs = sb("cross", [P, 2, H * CH])
            gram_ps, at_ok, at_dram, l_ok = sem("gram_psum"), sem("gram_rows"), sem("gram_stored"), sem("chunk_A_loaded")
            t_init, t_step, t_copy, t_dram, tt_ok, tt_zero = (sem("inv_init"), sem("inv_step"), sem("inv_copied"), sem("inv_stored"),
                                                              sem("inv_loaded"), sem("TT_zeroed"))
            psz, x_ps, x_sb, y_ps, y_sb = (sem("psum_zeroed"), sem("cross_psum"), sem("cross_sbuf"), sem("joined_psum"), sem("joined"))
            block = c1.enter_context(nc.Block())

            @block.tensor
            def _(pe):
                for c in range(NT):
                    if c >= 2:
                        pe.wait_ge(at_ok, 2 * (c - 1))
                    o = 4 * (c % 2)
                    for h in range(H):
                        gq, j = h // 4, h % 4
                        for b in range(B):
                            kt = g.KT[32 * j:32 * j + HD, gq, b, c * R:(c + 1) * R]
                            last = nc.tensor.matmul(ps[R * b:R * b + R, o + j, R * gq:R * gq + R], kt, kt, start=True, stop=True)
                    last.then_inc(gram_ps, 1)
                pe.wait_ge(psz, 1)
                pe.wait_ge(tt_ok, 16 * 12)
                pe.wait_ge(at_ok, 2 * NT)

                def cross(c):
                    if c >= 2:
                        pe.wait_ge(x_sb, c - 1)
                    for h in range(H):
                        for b in range(B):
                            a = AT[R * b:R * b + CH, c, :, h]
                            last = nc.tensor.matmul(ps[R * b:R * b + R, 4 + c % 2, h * CH:(h + 1) * CH], a,
                                                    TN[R * b:R * b + CH, c, :, h], start=True, stop=True)
                    last.then_inc(x_ps, 1)

                cross(0)
                for c in range(NT):
                    if c + 1 < NT:
                        cross(c + 1)
                    pe.wait_ge(x_sb, c + 1)
                    if c >= 2:
                        pe.wait_ge(y_sb, c - 1)
                    for h in range(H):
                        for b in range(B):
                            last = nc.tensor.matmul(ps[R * b:R * b + CH, 6 + c % 2, h * CH:(h + 1) * CH],
                                                    Xs[R * b:R * b + R, c % 2, h * CH:(h + 1) * CH],
                                                    TT[R * b:R * b + R, c, CH:R, h], start=True, stop=True)
                    last.then_inc(y_ps, 1)

            @block.vector
            def _(dve):
                for c in range(NT):
                    dve.wait_ge(gram_ps, c + 1)
                    o = 4 * (c % 2)
                    bt = g.beta[:, c, :]
                    for hf in range(2):
                        src = ps[:, o:o + 4, 0:P].rearrange("p j (q f i) -> p j q f i", q=HG, f=2)[:, :, :, hf, :]
                        dst = AT[:, c, CH * hf:CH * hf + CH, :].rearrange("p i (q j) -> p j q i", q=HG)
                        nc.vector.tensor_tensor(dst, src, bcast(bt, [[1, 4], [4, HG], [0, CH]]), ALU.mult).then_inc(at_ok, 1)
                dve.wait_ge(at_ok, 2 * NT)
                nc.vector.memset(ps[:, 6:8, :], 0.0).then_inc(psz, 1)
                dve.wait_ge(l_ok, 16 * 2 * B)
                dve.wait_ge(t_init, CH + 1)
                for j in range(CH - 1):
                    n_m, n_i = j + 1, CH - 1 - j
                    t = bcast(tmp[:, :], [[H * n_i, n_m], [H, n_i], [1, H]])
                    a = bcast(L[:, j, j + 1:, :], [[0, n_m], [H, n_i], [1, H]])
                    tj = bcast(T[:, 0:1, j:j + 1, :], [[H * CH, n_m], [0, n_i], [1, H]])
                    ti = T[:, 0:n_m, j + 1:, :]
                    if j:
                        dve.wait_ge(t_step, 2 * j)
                    nc.vector.tensor_tensor(t, a, tj, ALU.mult).then_inc(t_step, 1)
                    dve.wait_ge(t_step, 2 * j + 1)
                    nc.vector.tensor_tensor(ti, ti, t, ALU.subtract).then_inc(t_step, 1)
                for c in range(NT):
                    dve.wait_ge(y_ps, c + 1)
                    nc.vector.tensor_tensor(TT[:, c, CH:R, :], TT[:, c, CH:R, :], ps[:, 6 + c % 2, 0:H * CH].rearrange("p (h i) -> p i h", h=H),
                                            ALU.subtract).then_inc(y_sb, 1)

            @block.gpsimd
            def _(pool):
                nc.gpsimd.memset(T[:, :, :, :], 0.0).then_inc(t_init, 1)
                pool.wait_ge(t_init, 1)
                for m in range(CH):
                    nc.gpsimd.memset(T[:, m, m, :], 1.0).then_inc(t_init, 1)
                nc.gpsimd.memset(TT[:, :, :, :], 0.0).then_inc(tt_zero, 1)

            @block.scalar
            def _(act):
                act.wait_ge(t_step, 2 * (CH - 1))
                nc.scalar.copy(TC[:, :, :, :].rearrange("p i m h -> p m i h"), T[:, :, :, :]).then_inc(t_copy, 1)
                for c in range(NT):
                    act.wait_ge(x_ps, c + 1)
                    if c >= 2:
                        act.wait_ge(y_ps, c - 1)
                    nc.scalar.copy(Xs[:, c % 2, :], ps[:, 4 + c % 2, 0:H * CH]).then_inc(x_sb, 1)

            @block.sync
            def _(sp):
                W = H * CH
                sp.wait_ge(at_ok, 2 * NT)
                sp.dma_start(g.gram_d, AT[:, :, :, :].rearrange("p c i h -> p (c i h)")).then_inc(at_dram, 16)
                sp.wait_ge(at_dram, 16)
                for b in range(B):
                    for hf in range(2):
                        src = bass.AP(tensor=g.gram_d.tensor, offset=((R * b + CH * hf) * NT * 2 + hf) * W,
                                      ap=[[2 * W, NT], [2 * NT * W, CH], [1, W]])
                        p0 = 2 * NT * b + hf
                        sp.dma_start(L[p0:p0 + 2 * NT - 1:2, :, :, :].rearrange("p j i h -> p j (i h)"), src).then_inc(l_ok, 16)
                sp.wait_ge(t_step, 2 * (CH - 1))
                sp.dma_start(g.inv_d[0], T[:, :, :, :].rearrange("p m i h -> p (m i h)")).then_inc(t_dram, 16)
                sp.wait_ge(t_copy, 1)
                sp.dma_start(g.inv_d[1], TC[:, :, :, :].rearrange("p i m h -> p (i m h)")).then_inc(t_dram, 16)
                sp.wait_ge(t_dram, 32)
                sp.wait_ge(tt_zero, 1)
                for b in range(B):
                    for hf in range(2):
                        src = bass.AP(tensor=g.inv_d.tensor, offset=(2 * NT * b + hf) * CH * W,
                                      ap=[[W, CH], [2 * CH * W, NT], [1, W]])
                        sp.dma_start(TT[R * b + CH * hf:R * b + CH * hf + CH, :, CH * hf:CH * hf + CH, :].rearrange("p c i h -> p c (i h)"), src).then_inc(tt_ok, 16)
                    src = bass.AP(tensor=g.inv_d.tensor, offset=P * CH * W + 2 * NT * b * CH * W,
                                  ap=[[W, CH], [2 * CH * W, NT], [1, W]])
                    sp.dma_start(TN[R * b:R * b + CH, :, :, :].rearrange("p c m h -> p c (m h)"), src).then_inc(tt_ok, 16)

        sb = lambda n, s, d=F32: ctx.enter_context(nc.sbuf_tensor(n, s, d))
        TT = g.TT
        S = sb("state", [P, B, HG, HD])
        rhs = sb("scan_rhs", [P, D])
        NV = 4
        VA = sb("v_new", [P, NV, H, 2 * HD])
        z_ok, ks_ps, rhs_ok, vn_ps, vn_ok, su_ps, s_ok = (sem("scan_zeroed"), sem("KS_psum"), sem("rhs_rows"), sem("v_new_psum"),
                                                                  sem("v_new_rows"), sem("state_psum"), sem("state_ok"))
        va_out = [sem(f"v_new_stored{i}") for i in range(NV)]
        block = ctx.enter_context(nc.Block())

        @block.tensor
        def _(pe):
            pe.wait_ge(z_ok, 3)
            for c in range(NT):
                if c:
                    pe.wait_ge(s_ok, c)
                    for h in range(H):
                        gq, j = h // 4, h % 4
                        for b in range(B):
                            last = nc.tensor.matmul(ps[R * b:R * b + R, j, HD * gq:HD * gq + HD], g.KT[32 * j:32 * j + HD, gq, b, c * R:(c + 1) * R],
                                                    S[32 * j:32 * j + HD, b, gq, :], start=True, stop=True)
                    last.then_inc(ks_ps, 1)
                pe.wait_ge(rhs_ok, c + 1)
                for h in range(H):
                    for b in range(B):
                        last = nc.tensor.matmul(ps[R * b:R * b + R, 4, h * HD:(h + 1) * HD], TT[R * b:R * b + R, c, :, h],
                                                rhs[R * b:R * b + R, h * HD:(h + 1) * HD], start=True, stop=True)
                last.then_inc(vn_ps, 1)
                if c + 1 < NT:
                    pe.wait_ge(vn_ok, c + 1)
                    for b in range(B):
                        for h in range(H):
                            gq, j = h // 4, h % 4
                            last = nc.tensor.matmul(ps[32 * j:32 * j + HD, b, 64 + HD * gq:64 + HD * gq + HD], g.KB[R * b:R * b + R, c, h * HD:(h + 1) * HD],
                                                    VA[R * b:R * b + R, c % NV, h, 0:HD], start=True, stop=True)
                    last.then_inc(su_ps, 1)

        @block.vector
        def _(dve):
            nc.vector.memset(ps[:, 0:4, 0:P], 0.0).then_inc(z_ok, 1)
            nc.vector.memset(S[:, :, :, :], 0.0).then_inc(z_ok, 1)
            nc.vector.memset(VA[:, :, :, :], 1.0).then_inc(z_ok, 1)
            dve.wait_ge(z_ok, 3)
            for c in range(NT):
                if c:
                    dve.wait_ge(ks_ps, c)
                    nc.vector.tensor_tensor(rhs[:, :].rearrange("p (q j e) -> p j q e", q=HG, j=4), g.V[:, c, :].rearrange("p (q j e) -> p j q e", q=HG, j=4),
                                            ps[:, 0:4, 0:64].rearrange("p j (q e) -> p j q e", q=HG), ALU.subtract).then_inc(rhs_ok, 1)
                else:
                    nc.vector.tensor_copy(rhs[:, :], g.V[:, 0, :]).then_inc(rhs_ok, 1)
                dve.wait_ge(vn_ps, c + 1)
                if c >= NV:
                    dve.wait_ge(va_out[c % NV], 64 * (c // NV))
                nc.vector.tensor_copy(VA[:, c % NV, :, 0:HD], ps[:, 4, 0:D].rearrange("p (h e) -> p h e", h=H)).then_inc(vn_ok, 1)
                if c + 1 < NT:
                    dve.wait_ge(su_ps, c + 1)
                    nc.vector.tensor_tensor(S[:, :, :, :], S[:, :, :, :], ps[:, 0:4, 64:P].rearrange("p b (q e) -> p b q e", q=HG), ALU.add).then_inc(s_ok, 1)
                if c + 1 < NT:
                    dve.wait_ge(s_ok, c + 1)

        @block.sync
        def _(sp):
            for c in range(NT):
                sp.wait_ge(vn_ok, c + 1)
                for b in range(B):
                    i0 = R * (c % 4)
                    sp.dma_start(g.VN[i0:i0 + R, b, c // 4, :], VA[R * b:R * b + R, c % NV, :, :].rearrange("p h e -> p (h e)")).then_inc(va_out[c % NV], 16)
            for i in range(NV):
                sp.wait_ge(va_out[i], 64 * NT // NV)


MAX_UNITS = [(0, 4 * i, 4) for i in range(4)] + [(1, 2 * i, 2) for i in range(8)] + [(t, h, 1) for t in (2, 3) for h in range(H)]
NMU = len(MAX_UNITS)
STEPS = HG * 3 * 2
KEYS = [[(0, 0)], [(1, 0)], [(2, 0), (3, 256)]]
WIDTH = [512, 384, 384]


def max_units_at(step):
    last = STEPS - 2
    return range(NMU * step // last, NMU * (step + 1) // last) if step < last else range(0)


def phase_attention(nc, g, name, OT, shared_k, parts_k, k_row0, va):
    with ExitStack() as ctx:
        sb = lambda n, s, d=F32: ctx.enter_context(nc.sbuf_tensor(f"{name}_{n}", s, d))
        sem = semaphores(nc, ctx, f"{name}_")
        ps = g.ps
        NS = 3
        HK = 1 if shared_k else H
        QS = sb("q_stack", [P, NS, H, N], BF16)
        KS = sb("k_stack", [P, NS, HK, N], BF16)
        PT = sb("probs", [P, 4, 2, N])
        mx = sb("neg_max", [P, 4, H])
        mrem = sb("max_rem", [P, 4, H])
        mp = sb("max_parts", [P, 4, NPART, H], BF16)
        mT = sb("max_partsT", [NPART * H, N], BF16)
        stack = [sem(f"stack_loaded{i}") for i in range(NS)]
        mrow = [sem(f"max_rows_loaded{i}") for i in range(NS)]
        ones_ok, mu_ps, mu_ok, mp_ok, mt_ps, mt_sb = (sem("ones_rows"), sem("max_unit_psum"), sem("max_unit_reduced"), sem("max_parts"),
                                                      sem("maxT_psum"), sem("maxT_sbuf"))
        st_ps, exp_ok, pv_ok, ot_sb = sem("scoresT_psum"), sem("probs_ready"), sem("pv_done"), sem("out_group_sbuf")
        block = ctx.enter_context(nc.Block())

        def pv_at(S):
            return [(S - 3) // 2] if S >= 3 and S % 2 == 1 else []

        @block.sync
        def _(sp):
            for b in range(B):
                s = b % NS
                if b >= NS:
                    sp.wait_ge(st_ps, STEPS * (b - NS + 1))
                for r, (pq, pk) in enumerate(PAIRS):
                    src = bass.AP(tensor=g.parts_d.tensor, offset=pq * 4 * P * B * N + b * N, ap=[[B * N, HD], [HD * B * N, H], [1, N]])
                    sp.dma_start(QS[HD * r:HD * r + HD, s, :, :], src).then_inc(stack[s], 16)
                    src = bass.AP(tensor=parts_k.tensor, offset=(pk * 4 * P + k_row0) * B * N + b * N, ap=[[B * N, HD], [HD * B * N, HK], [1, N]])
                    sp.dma_start(KS[HD * r:HD * r + HD, s, :, :], src).then_inc(stack[s], 16)

        @block.gpsimd
        def _(pool):
            nc.gpsimd.memset(KS[KR:KRM, :, :, :], 1.0).then_inc(ones_ok, 1)
            for b in range(B):
                s = b % NS
                pool.wait_ge(mt_sb, b + 1)
                for p in range(NPART):
                    pool.dma_start(QS[KR + p:KR + p + 1, s, :, :], mT[H * p:H * p + H, :]).then_inc(mrow[s], 16)

        @block.tensor
        def _(pe):
            def max_unit(b, u):
                n = b * (NMU + 1) + u
                bank, s = n % 2, b % NS
                if u == 0:
                    pe.wait_ge(stack[s], 16 * 2 * len(PAIRS) * (b // NS + 1))
                if u >= 2:
                    pe.wait_ge(mu_ok, b * NMU + u - 1)
                elif b:
                    if u == 0:
                        pe.wait_ge(mu_ok, b * NMU)
                    else:
                        pe.wait_ge(mt_sb, b)
                if u == NMU:
                    pe.wait_ge(mp_ok, 4 * (b + 1))
                    out = ps[:, bank, :].bitcast(BF16)
                    for t in range(4):
                        last = nc.tensor.transpose(out[0:NPART * H, t * P:(t + 1) * P], mp[:, t, :, :].rearrange("p a h -> p (a h)"), g.idb[:, :])
                    last.then_inc(mt_ps, 1)
                    return
                t, h0, nh = MAX_UNITS[u]
                w = (t + 1) * P
                for h in range(h0, h0 + nh):
                    o = (h - h0) * w
                    kh = 0 if shared_k else h
                    nc.tensor.matmul(ps[:, bank, o:o + w], QS[0:KR, s, h, t * P:(t + 1) * P], KS[0:KR, s, kh, 0:w], start=True, stop=False)
                    last = nc.tensor.matmul(ps[:, bank, o + w - P:o + w], g.idb[:, :], g.maskq[:, :], start=False, stop=True)
                last.then_inc(mu_ps, 1)

            def score_unit(S):
                b, s = S // STEPS, S // STEPS % NS
                gq, ks, pr = S % STEPS // 6, S % 6 // 2, S % 2
                if S % STEPS == 0:
                    pe.wait_ge(mrow[s], 48 * (b // NS + 1))
                if S >= 2:
                    pe.wait_ge(exp_ok, S - 1)
                for e in range(2):
                    h = 4 * gq + 2 * pr + e
                    kh = 0 if shared_k else h
                    for kb, o in KEYS[ks]:
                        w = N - kb * P
                        bank = 2 + 2 * (S % 2) + e
                        nc.tensor.matmul(ps[:, bank, o:o + w], KS[0:KRM, s, kh, kb * P:(kb + 1) * P], QS[0:KRM, s, h, kb * P:N], start=True, stop=False)
                        last = nc.tensor.matmul(ps[:, bank, o:o + P], g.idb[:, :], g.maskk[:, :], start=False, stop=True)
                last.then_inc(st_ps, 1)

            def pv(n):
                og, ks = n // 3, n % 3
                b, gq = og // HG, og % HG
                pe.wait_ge(exp_ok, 2 * (n + 1))
                if ks == 0 and og >= 2:
                    pe.wait_ge(ot_sb, og - 1)
                for kb, o in KEYS[ks]:
                    w = N - kb * P
                    for j in range(4):
                        slot = (2 * n + j // 2) % 4
                        last = nc.tensor.matmul(ps[32 * j:32 * j + 32, 6 + og % 2, kb * P:N], va(b, kb, 4 * gq + j),
                                                PT[:, slot, j % 2, o:o + w], start=(kb == 0), stop=(kb == 3))
                last.then_inc(pv_ok, 1)

            pe.wait_ge(ones_ok, 1)
            for u in range(NMU + 1):
                max_unit(0, u)
            for S in range(B * STEPS):
                score_unit(S)
                for n in pv_at(S):
                    pv(n)
                if S // STEPS + 1 < B:
                    for u in max_units_at(S % STEPS):
                        max_unit(S // STEPS + 1, u)
                    if S % STEPS == STEPS - 1:
                        max_unit(S // STEPS + 1, NMU)
            pv(B * STEPS // 2 - 1)

        @block.vector
        def _(dve):
            def reduce_unit(b, u):
                t, h0, nh = MAX_UNITS[u]
                w = (t + 1) * P
                dve.wait_ge(mu_ps, b * NMU + u + 1)
                if b and u == 0:
                    dve.wait_ge(mp_ok, 4 * b)
                nc.vector.tensor_reduce(mx[:, t, h0:h0 + nh], ps[:, (b * (NMU + 1) + u) % 2, 0:nh * w].rearrange("p (h k) -> p h k", h=nh),
                                        AX.X, ALU.max, negate=True).then_inc(mu_ok, 1)

            def split_max(b):
                dve.wait_ge(mu_ok, NMU * (b + 1))
                if b:
                    dve.wait_ge(mt_ps, b)
                nc.vector.tensor_copy(mp[:, :, 0, :], mx[:, :, :]).then_inc(mp_ok, 1)
                dve.wait_ge(mp_ok, 4 * b + 1)
                nc.vector.tensor_tensor(mrem[:, :, :], mx[:, :, :], mp[:, :, 0, :], ALU.subtract).then_inc(mp_ok, 1)
                dve.wait_ge(mp_ok, 4 * b + 2)
                nc.vector.tensor_copy(mp[:, :, 1, :], mrem[:, :, :]).then_inc(mp_ok, 1)
                dve.wait_ge(mp_ok, 4 * b + 3)
                nc.vector.tensor_tensor(mp[:, :, 2, :], mrem[:, :, :], mp[:, :, 1, :], ALU.subtract).then_inc(mp_ok, 1)

            def out_group(n):
                og = n // 3
                b, gq = og // HG, og % HG
                dve.wait_ge(pv_ok, n + 1)
                nc.vector.tensor_copy(OT[:, gq, :, R * b:R * b + R], ps[:, 6 + og % 2, :].rearrange("p (c i) -> p c i", c=NT)).then_inc(ot_sb, 1)

            for u in range(NMU):
                reduce_unit(0, u)
            split_max(0)
            for S in range(B * STEPS):
                if S // STEPS + 1 < B:
                    for u in max_units_at(S % STEPS):
                        reduce_unit(S // STEPS + 1, u)
                    if S % STEPS == STEPS - 2:
                        split_max(S // STEPS + 1)
                for n in pv_at(S):
                    if n % 3 == 2:
                        out_group(n)
            out_group(B * STEPS // 2 - 1)

        @block.scalar
        def _(act):
            def maxT(b):
                act.wait_ge(mt_ps, b + 1)
                if b:
                    act.wait_ge(mrow[(b - 1) % NS], 48 * ((b - 1) // NS + 1))
                nc.scalar.copy(mT[:, :], ps[:, (b * (NMU + 1) + NMU) % 2, :].bitcast(BF16)[0:NPART * H, 0:N]).then_inc(mt_sb, 1)

            maxT(0)
            for S in range(B * STEPS):
                n = S // 2
                act.wait_ge(st_ps, S + 1)
                if S >= 4:
                    act.wait_ge(pv_ok, n - 1)
                w = WIDTH[S % 6 // 2]
                bank = 2 + 2 * (S % 2)
                nc.scalar.activation(PT[:, S % 4, :, 0:w], ps[:, bank:bank + 2, 0:w], ACT.Exp, scale=SCALE).then_inc(exp_ok, 1)
                if S // STEPS + 1 < B and S % STEPS == STEPS - 1:
                    maxT(S // STEPS + 1)


class LayerNorm:

    def __init__(self, nc, ctx, name, half):
        self.nc = nc
        sb = lambda n, s: ctx.enter_context(nc.sbuf_tensor(f"{name}_{n}", s, F32))
        sem = semaphores(nc, ctx, f"{name}_")
        self.half = half
        self.st, self.mv, self.rs = sb("stats", [P, 4, 6]), sb("mean_var", [P, 4, 2]), sb("rstd", [P, 4, 1])
        self.st_ok, self.mv_ok, self.rs_ok, self.y_ok = sem("stats_ok"), sem("mean_var_ok"), sem("rstd_ok"), sem("normalized")

    def stats(self, dve, n, x):
        nc, s = self.nc, n % 4
        nc.vector.bn_stats(self.st[:, s, :], x).then_inc(self.st_ok, 1)
        dve.wait_ge(self.st_ok, n + 1)
        if n >= 4:
            dve.wait_ge(self.y_ok, n - 3)
        nc.vector.bn_aggr(self.mv[:, s, :], self.st[:, s, :]).then_inc(self.mv_ok, 1)

    def rstd(self, pool, n):
        nc, s = self.nc, n % 4
        pool.wait_ge(self.mv_ok, n + 1)
        if n >= 4:
            pool.wait_ge(self.y_ok, n - 3)
        nc.gpsimd.tensor_scalar(self.rs[:, s, :], self.mv[:, s, 1:2], 1.0, EPS_LN, ALU.mult, ALU.add).then_inc(self.rs_ok, 1)
        pool.wait_ge(self.rs_ok, 2 * n + 1)
        nc.gpsimd.tensor_tensor(self.rs[:, s, :], self.rs[:, s, :], self.half[:, 0:1], ALU.pow).then_inc(self.rs_ok, 1)

    def apply(self, dve, n, out, x):
        nc, s = self.nc, n % 4
        dve.wait_ge(self.rs_ok, 2 * n + 2)
        nc.vector.tensor_scalar(out, x, self.mv[:, s, 0:1], self.rs[:, s, :], ALU.subtract, ALU.mult).then_inc(self.y_ok, 1)


def phase_out_proj(nc, g, name, OT, load_w, bias):
    with ExitStack() as ctx:
        sb = lambda n, s, d=F32: ctx.enter_context(nc.sbuf_tensor(f"{name}_{n}", s, d))
        sem = semaphores(nc, ctx, f"{name}_")
        ps = g.ps
        rec = sb("inv_sum", [P, 2, H])
        on = sb("heads", [P, 2, D])
        onT = sb("headsT", [P, 2, KD, P])
        o_ps, rec_ok, on_ok, t_ps, t_sb, y_ps, u_ok, b_ok = (sem("rows_psum"), sem("inv_sum_ok"), sem("heads_ok"), sem("headsT_psum"), sem("headsT_sbuf"),
                                                           sem("proj_psum"), sem("residual_added"), sem("bias_added"))
        w_ld = sem("w_loaded")
        ln = LayerNorm(nc, ctx, name, g.mhalf)
        W = load_w(None, None)
        block = ctx.enter_context(nc.Block())

        @block.sync
        def _(sp):
            load_w(sp, w_ld)

        @block.tensor
        def _(pe):
            def rows(c):
                if c >= 2:
                    pe.wait_ge(on_ok, c - 1)
                for q in range(HG):
                    last = nc.tensor.transpose(ps[:, c % 2, q * P:(q + 1) * P], OT[:, q, c, :], g.idf[:, :])
                last.then_inc(o_ps, 1)

            def headsT(c):
                pe.wait_ge(on_ok, c + 1)
                if c >= 2:
                    pe.wait_ge(t_sb, c - 1)
                for k in range(KD):
                    last = nc.tensor.transpose(ps[:, 2 + c % 2, k * P:(k + 1) * P], on[:, c % 2, k * P:(k + 1) * P], g.idf[:, :])
                last.then_inc(t_ps, 1)

            def project(c):
                if c == 0:
                    pe.wait_ge(w_ld, 16)
                pe.wait_ge(t_sb, c + 1)
                if c >= 2:
                    pe.wait_ge(u_ok, c - 1)
                for k in range(KD):
                    last = nc.tensor.matmul(ps[:, 4 + c % 2, 0:D], onT[:, c % 2, k, :], W[:, k, :], start=(k == 0), stop=(k == KD - 1))
                last.then_inc(y_ps, 1)

            rows(0)
            for c in range(NT):
                if c + 1 < NT:
                    rows(c + 1)
                headsT(c)
                if c:
                    project(c - 1)
            project(NT - 1)

        @block.vector
        def _(dve):
            def heads(c):
                dve.wait_ge(o_ps, c + 1)
                if c >= 2:
                    dve.wait_ge(t_ps, c - 1)
                v = ps[:, c % 2, :].rearrange("p (h e) -> p h e", h=H)
                nc.vector.reciprocal(rec[:, c % 2, :], v[:, :, HD]).then_inc(rec_ok, 1)
                dve.wait_ge(rec_ok, c + 1)
                nc.vector.tensor_tensor(on[:, c % 2, :].rearrange("p (h e) -> p h e", h=H), v[:, :, 0:HD],
                                        bcast(rec[:, c % 2, :], [[1, H], [0, HD]]), ALU.mult).then_inc(on_ok, 1)

            def residual(c):
                dve.wait_ge(y_ps, c + 1)
                if bias is not None:
                    dve.wait_ge(b_ok, c + 1)
                nc.vector.tensor_tensor(g.X[:, c, :], g.X[:, c, :], ps[:, 4 + c % 2, 0:D], ALU.add).then_inc(u_ok, 1)
                dve.wait_ge(u_ok, c + 1)
                ln.stats(dve, c, g.X[:, c, :])

            for c in range(NT + 3):
                if c < NT:
                    heads(c)
                if 2 <= c < NT + 2:
                    residual(c - 2)
                if c >= 3:
                    ln.apply(dve, c - 3, g.X[:, c - 3, :], g.X[:, c - 3, :])

        @block.scalar
        def _(act):
            for c in range(NT):
                act.wait_ge(t_ps, c + 1)
                if c >= 2:
                    act.wait_ge(y_ps, c - 1)
                nc.scalar.copy(onT[:, c % 2, :, :], ps[:, 2 + c % 2, 0:KD * P].rearrange("p (k m) -> p k m", k=KD)).then_inc(t_sb, 1)

        @block.gpsimd
        def _(pool):
            if bias is not None:
                for c in range(NT):
                    nc.gpsimd.tensor_tensor(g.X[:, c, :], g.X[:, c, :], bias[:, :], ALU.add).then_inc(b_ok, 1)
            for c in range(NT):
                ln.rstd(pool, c)


def phase_weights(nc, g):
    F4 = 4 * D
    KF = F4 // P
    with ExitStack() as ctx:
        sb = lambda n, s, d=F32: ctx.enter_context(nc.sbuf_tensor(f"wt_{n}", s, d))
        sem = semaphores(nc, ctx, f"wt_")
        ps = g.ps
        ew, epw = sb("ent_w", [P, 2, KD, F4]), sb("ent_pw", [P, 2, KF, D])
        ewT = sb("ent_wT", [P, 2, KF, D])
        eb, ebT = sb("ent_b", [2 * KF, P]), sb("ent_bT", [P, 2 * KF])
        pw = sb("path_w", [P, 2, 2, KD, D])
        ph, kk, pb = sb("phase", [P, 2, 4 * D]), sb("turns", [P, 4 * D]), sb("path_b", [P, 4 * D])
        ld, ldp, mod_st, sin_ok, tp, te, wp, we, pth = (sem("loaded"), sem("phase_loaded"), sem("modulation"), sem("sines"), sem("transposed"),
                                                        sem("evacuated"), sem("product"), sem("product_out"), sem("paths"))
        block = ctx.enter_context(nc.Block())
        d = g.d

        @block.sync
        def _(sp):
            sp.dma_start(ph[:, 0, :], rows_bcast(d["L0_ffn_phase"], 0, 4 * D)).then_inc(ldp, 16)
            for l in range(2):
                sp.dma_start(ew[:, l, :, :], d["L0_ffn_ent_w"][l].rearrange("(k p) n -> p k n", p=P)).then_inc(ld, 16)
                sp.dma_start(epw[:, l, :, :], d["L0_ffn_ent_pw"][l].rearrange("(k p) n -> p k n", p=P)).then_inc(ld, 16)
                for q in range(2):
                    sp.dma_start(pw[:, l, q, :, :], d["L0_ffn_path_w"][l, q].rearrange("(k p) n -> p k n", p=P)).then_inc(ld, 16)
            sp.dma_start(eb[:, :], d["L0_ffn_ent_b"].rearrange("l (k p) -> (l k) p", p=P)).then_inc(ld, 16)
            sp.dma_start(pb[:, :], rows_bcast(d["L0_ffn_path_b"], 0, 4 * D)).then_inc(ld, 16)
            sp.dma_start(g.Wap[:, :, 0:D], d["L0_ffn_amp_w"].rearrange("(k p) n -> p k n", p=P)).then_inc(ld, 16)
            sp.dma_start(g.Wap[:, :, D:], d["L0_ffn_ph_w"].rearrange("(k p) n -> p k n", p=P)).then_inc(ld, 16)
            sp.dma_start(g.bap[:, 0:D], rows_bcast(d["L0_ffn_amp_b"], 0, D)).then_inc(ld, 16)
            sp.dma_start(g.bap[:, D:], rows_bcast(d["L0_ffn_ph_b"], 0, D)).then_inc(ld, 16)
            for l in range(2):
                sp.dma_start(g.bst[:, 2 * l, :], rows_bcast(d["L0_ffn_ent_pb"], l * D, D)).then_inc(ld, 16)
                for s, (gm, bt) in enumerate((("ln3_g", "ln3_b"), ("ln4_g", "ln4_b"))):
                    sp.dma_start(g.gam[:, 2 * l + s, :], rows_bcast(d["L0_ffn_" + gm], l * D, D)).then_inc(ld, 16)
                    sp.dma_start(g.bet[:, 2 * l + s, :], rows_bcast(d["L0_ffn_" + bt], l * D, D)).then_inc(ld, 16)

        NLD = 8 + 6 + 10

        @block.vector
        def _(dve):
            p0, p1 = ph[:, 0, :], ph[:, 1, :]
            n = [0]

            def step(ins):
                n[0] += 1
                ins.then_inc(mod_st, 1)
                dve.wait_ge(mod_st, n[0])

            dve.wait_ge(ldp, 16)
            MAGIC = 12582912.0
            step(nc.vector.tensor_scalar(kk[:, :], p0, 1.0 / (2 * PI), None, ALU.mult))
            step(nc.vector.tensor_scalar(kk[:, :], kk[:, :], MAGIC, None, ALU.add))
            step(nc.vector.tensor_scalar(kk[:, :], kk[:, :], -MAGIC, None, ALU.add))
            c1 = 6.28125
            c2 = float((np.array([2 * PI - c1], np.float32).view(np.uint32) & np.uint32(0xFFFFF000)).view(np.float32)[0])
            c3 = 2 * PI - c1 - c2
            for cc in (c1, c2, c3):
                step(nc.vector.scalar_tensor_tensor(out=p0, in0=kk[:, :], scalar=-cc, in1=p0, op0=ALU.mult, op1=ALU.add))
            step(nc.vector.tensor_scalar(p0, p0, 3.1415925, -3.1415925, ALU.min, ALU.max))
            step(nc.vector.scalar_tensor_tensor(out=p1, in0=p0, scalar=-1.0, in1=p0, op0=ALU.mult, op1=ALU.min))
            step(nc.vector.tensor_scalar(p1, p1, PI / 2, None, ALU.add))
            dve.wait_ge(sin_ok, 1)
            step(nc.vector.tensor_tensor(p0, p0, p1, ALU.add))
            dve.wait_ge(ld, 16 * NLD)
            for l in range(2):
                mod = [p0[:, (2 * l + q) * D:(2 * l + q + 1) * D] for q in range(2)]
                for q in range(2):
                    step(nc.vector.tensor_tensor(pw[:, l, q, :, :], pw[:, l, q, :, :], bcast(mod[q], [[0, KD], [1, D]]), ALU.mult))
                step(nc.vector.tensor_tensor(g.Wst[:, 2 * l + 1, :, :], pw[:, l, 0, :, :], pw[:, l, 1, :, :], ALU.add))
            step(nc.vector.tensor_tensor(pb[:, :], pb[:, :], p0, ALU.mult))
            for l in range(2):
                step(nc.vector.tensor_tensor(g.bst[:, 2 * l + 1, :], pb[:, 2 * l * D:(2 * l + 1) * D], pb[:, (2 * l + 1) * D:(2 * l + 2) * D], ALU.add))
            for l in range(2):
                dve.wait_ge(wp, 3 * l + 3)
                for k in range(KD):
                    nc.vector.tensor_copy(g.Wst[:, 2 * l, k, :], ps[:, 4 + k, 0:D]).then_inc(we, 1)
                nc.vector.tensor_tensor(g.bst[:, 2 * l, :], g.bst[:, 2 * l, :], ps[:, 6, 0:D], ALU.add).then_inc(we, 1)

        @block.scalar
        def _(act):
            act.wait_ge(mod_st, 9)
            nc.scalar.activation(ph[:, :, :], ph[:, :, :], ACT.Sin).then_inc(sin_ok, 1)
            for i in range(2 * KF + 1):
                act.wait_ge(tp, i + 1)
                if i < 2 * KF:
                    l, k = i // KF, i % KF
                    nc.scalar.copy(ewT[:, l, k, :], ps[:, i % 4, 0:D]).then_inc(te, 1)
                else:
                    nc.scalar.copy(ebT[:, :], ps[:, i % 4, 0:2 * KF]).then_inc(te, 1)

        @block.tensor
        def _(pe):
            pe.wait_ge(ld, 16 * NLD)
            for i in range(2 * KF + 1):
                if i >= 4:
                    pe.wait_ge(te, i - 3)
                if i < 2 * KF:
                    l, k = i // KF, i % KF
                    for m in range(KD):
                        last = nc.tensor.transpose(ps[:, i % 4, m * P:(m + 1) * P], ew[:, l, m, k * P:(k + 1) * P], g.idf[:, :])
                else:
                    last = nc.tensor.transpose(ps[:, i % 4, 0:2 * KF], eb[:, :], g.idf[0:2 * KF, 0:2 * KF])
                last.then_inc(tp, 1)
            pe.wait_ge(te, 2 * KF + 1)
            for l in range(2):
                if l:
                    pe.wait_ge(we, 3)
                for m in range(KD):
                    for k in range(KF):
                        last = nc.tensor.matmul(ps[:, 4 + m, 0:D], ewT[:, l, k, m * P:(m + 1) * P], epw[:, l, k, :], start=(k == 0), stop=(k == KF - 1))
                    last.then_inc(wp, 1)
                for k in range(KF):
                    last = nc.tensor.matmul(ps[:, 6, 0:D], bcast(ebT[:, l * KF + k:l * KF + k + 1], [[0, P]]), epw[:, l, k, :], start=(k == 0), stop=(k == KF - 1))
                last.then_inc(wp, 1)


def phase_ffn(nc, g):
    with ExitStack() as ctx:
        sb = lambda n, s, d=F32: ctx.enter_context(nc.sbuf_tensor(f"ffn_{n}", s, d))
        sem = semaphores(nc, ctx, f"ffn_")
        ps = g.ps
        ST = 4
        xT = sb("xT", [P, 4, KD, P])
        Z = sb("amp_phase", [P, NT, 2 * D])
        Hh = sb("h_rows", [P, NT, D])
        tb = sb("cos_arg", [P, 2, G4, D])
        hb = sb("residual", [P, 4, D])
        pih = sb("half_pi", [P, 1])
        t_ps, t_sb, z_ps, z_ok, sg_ok, ar_ok, sn_ok, h0_ok, c_ok = (sem("xT_psum"), sem("xT_sbuf"), sem("z_psum"), sem("z_rows"), sem("sigmoid_tanh"),
                                                                  sem("sine_args"), sem("sines"), sem("h_sum"), sem("const"))
        hb_ok, y_ps, u_ok, sc_ok, h_ok, fx_ok = (sem("h_plus_bias"), sem("y_psum"), sem("u_ok"), sem("scaled"), sem("h_ok"), sem("x_plus_h"))
        ln = LayerNorm(nc, ctx, "ffnln", g.mhalf)
        block = ctx.enter_context(nc.Block())
        NH = ST * NT

        @block.tensor
        def _(pe):
            def xpose(n):
                if n >= 2:
                    pe.wait_ge(t_sb, n - 1)
                if n < NT:
                    src = g.X[:, n, :]
                elif n < 2 * NT:
                    pe.wait_ge(h0_ok, 2 * ((n - NT) // G4 + 1))
                    src = Hh[:, n - NT, :]
                else:
                    pe.wait_ge(h_ok, n - 2 * NT + 1)
                    src = Hh[:, n % NT, :]
                for k in range(KD):
                    last = nc.tensor.transpose(ps[:, n % 2, k * P:(k + 1) * P], src[:, k * P:(k + 1) * P], g.idf[:, :])
                last.then_inc(t_ps, 1)

            def dense(n):
                pe.wait_ge(t_sb, n + 1)
                if n < NT:
                    if n >= 2:
                        pe.wait_ge(z_ok, n - 1)
                    for k in range(KD):
                        last = nc.tensor.matmul(ps[:, 2 + n % 2, :], xT[:, n % 4, k, :], g.Wap[:, k, :], start=(k == 0), stop=(k == KD - 1))
                    last.then_inc(z_ps, 1)
                else:
                    m = n - NT
                    if m >= 4:
                        pe.wait_ge(u_ok, m - 3)
                    for k in range(KD):
                        last = nc.tensor.matmul(ps[:, 4 + m % 4, 0:D], xT[:, n % 4, k, :], g.Wst[:, m // NT, k, :], start=(k == 0), stop=(k == KD - 1))
                    last.then_inc(y_ps, 1)

            xpose(0)
            for n in range(NT + NH):
                if n + 1 < NT + NH and n != NT - 1:
                    xpose(n + 1)
                dense(n)
                if n == NT - 1:
                    xpose(NT)

        @block.scalar
        def _(act):
            def evac(n):
                act.wait_ge(t_ps, n + 1)
                if 4 <= n < NT + 4:
                    act.wait_ge(z_ps, n - 3)
                elif n >= NT + 4:
                    act.wait_ge(y_ps, n - NT - 3)
                nc.scalar.copy(xT[:, n % 4, :, :], ps[:, n % 2, 0:KD * P].rearrange("p (k m) -> p k m", k=KD)).then_inc(t_sb, 1)

            for n in range(NT):
                evac(n)
            for q in range(NG):
                gs = slice(q * G4, (q + 1) * G4)
                act.wait_ge(z_ok, (q + 1) * G4)
                nc.scalar.activation(Z[:, gs, 0:D], Z[:, gs, 0:D], ACT.Sigmoid).then_inc(sg_ok, 1)
                nc.scalar.activation(Z[:, gs, D:], Z[:, gs, D:], ACT.Tanh).then_inc(sg_ok, 1)
            act.wait_ge(c_ok, 1)
            for q in range(NG):
                gs = slice(q * G4, (q + 1) * G4)
                act.wait_ge(ar_ok, 2 * (q + 1))
                nc.scalar.activation(Z[:, gs, D:], Z[:, gs, D:], ACT.Sin).then_inc(sn_ok, 1)
                nc.scalar.activation(tb[:, q % 2, :, :], tb[:, q % 2, :, :], ACT.Sin, bias=pih[:, 0:1]).then_inc(sn_ok, 1)
            for n in range(NT, NT + NH):
                evac(n)

        @block.vector
        def _(dve):
            nc.vector.memset(pih[:, :], PI / 2).then_inc(c_ok, 1)
            for n in range(NT):
                dve.wait_ge(z_ps, n + 1)
                nc.vector.tensor_tensor(Z[:, n, :], ps[:, 2 + n % 2, :], g.bap[:, :], ALU.add).then_inc(z_ok, 1)
            for q in range(NG):
                gs = slice(q * G4, (q + 1) * G4)
                dve.wait_ge(sg_ok, 2 * (q + 1))
                nc.vector.tensor_scalar(Z[:, gs, D:], Z[:, gs, D:], 3.1415925, None, ALU.mult).then_inc(ar_ok, 1)
                dve.wait_ge(ar_ok, 2 * q + 1)
                if q >= 2:
                    dve.wait_ge(h0_ok, 2 * (q - 1))
                nc.vector.scalar_tensor_tensor(out=tb[:, q % 2, :, :], in0=Z[:, gs, D:], scalar=-1.0, in1=Z[:, gs, D:], op0=ALU.mult, op1=ALU.min).then_inc(ar_ok, 1)

            def residual(m):
                if m < NH:
                    dve.wait_ge(y_ps, m + 1)
                    dve.wait_ge(hb_ok, m + 1)
                    nc.vector.tensor_tensor(hb[:, m % 4, :], hb[:, m % 4, :], ps[:, 4 + m % 4, 0:D], ALU.add).then_inc(u_ok, 1)
                    dve.wait_ge(u_ok, m + 1)
                    ln.stats(dve, m, hb[:, m % 4, :])
                else:
                    dve.wait_ge(fx_ok, m - NH + 1)
                    ln.stats(dve, m, g.X[:, m - NH, :])

            def normalize(m):
                x = hb[:, m % 4, :] if m < NH else g.X[:, m - NH, :]
                ln.apply(dve, m, x, x)

            for m in range(NH + NT + 1):
                if m < NH + NT:
                    residual(m)
                if m:
                    normalize(m - 1)

        @block.gpsimd
        def _(pool):
            for q in range(NG):
                gs = slice(q * G4, (q + 1) * G4)
                pool.wait_ge(sn_ok, 2 * (q + 1))
                nc.gpsimd.tensor_tensor(tb[:, q % 2, :, :], tb[:, q % 2, :, :], Z[:, gs, D:], ALU.add).then_inc(h0_ok, 1)
                pool.wait_ge(h0_ok, 2 * q + 1)
                nc.gpsimd.tensor_tensor(Hh[:, gs, :], tb[:, q % 2, :, :], Z[:, gs, 0:D], ALU.mult).then_inc(h0_ok, 1)

            def add_bias(m):
                if m >= 4:
                    pool.wait_ge(sc_ok, m - 3)
                if m < NT:
                    pool.wait_ge(h0_ok, 2 * (m // G4 + 1))
                else:
                    pool.wait_ge(h_ok, m - NT + 1)
                nc.gpsimd.tensor_tensor(hb[:, m % 4, :], Hh[:, m % NT, :], g.bst[:, m // NT, :], ALU.add).then_inc(hb_ok, 1)

            def scale(m):
                pool.wait_ge(ln.y_ok, m + 1)
                pool.wait_ge(t_ps, NT + m + 1)
                if m >= NT:
                    pool.wait_ge(hb_ok, m + 1)
                nc.gpsimd.tensor_tensor(Hh[:, m % NT, :], hb[:, m % 4, :], g.gam[:, m // NT, :], ALU.mult).then_inc(sc_ok, 1)
                pool.wait_ge(sc_ok, m + 1)
                nc.gpsimd.tensor_tensor(Hh[:, m % NT, :], Hh[:, m % NT, :], g.bet[:, m // NT, :], ALU.add).then_inc(h_ok, 1)

            def final_sum(c):
                pool.wait_ge(h_ok, NH - NT + c + 1)
                nc.gpsimd.tensor_tensor(g.X[:, c, :], g.X[:, c, :], Hh[:, c, :], ALU.add).then_inc(fx_ok, 1)

            for m in range(2):
                add_bias(m)
            for m in range(NH):
                if m + 2 < NH:
                    add_bias(m + 2)
                ln.rstd(pool, m)
                if m:
                    scale(m - 1)
                    if m > NH - NT:
                        final_sum(m - 1 - (NH - NT))
            for c in range(NT):
                ln.rstd(pool, NH + c)
                if c == 0:
                    scale(NH - 1)
                    final_sum(NT - 1)


def phase_l1_qkv(nc, g):
    with ExitStack() as ctx:
        sb = lambda n, s, d=F32: ctx.enter_context(nc.sbuf_tensor(f"l1q_{n}", s, d))
        sem = semaphores(nc, ctx, f"l1q_")
        ps = g.ps
        NO = D + 2 * HD
        ca = sb("c_attn", [P, 3, D])
        caT = sb("c_attnT", [P, KD, NO])
        cp = sb("c_proj", [P, KD, D])
        xT = sb("xT", [P, KD, B, N])
        qb, kb_, vb = sb("q_bias", [P, KD]), sb("k_bias", [HD, 1]), sb("v_bias", [P, HD])
        part = [sb(f"part{p}", [P, 3, B * N], BF16) for p in range(NPART)]
        rem = sb("rem", [P, 2, N])
        ld, w_ps, w_sb, t_ps, t_sb, q_ps, p1_ok, r_ok, p2_ok, p3_ok, st, v_ps, v_ok, one = (
            sem("loaded"), sem("wT_psum"), sem("wT_sbuf"), sem("xT_psum"), sem("xT_sbuf"), sem("qT_psum"), sem("part1"), sem("rem1"),
            sem("part2"), sem("part3"), sem("stored"), sem("v_psum"), sem("v_ok"), sem("ones"))
        block = ctx.enter_context(nc.Block())
        d = g.d
        OUT = [(0, P, 0), (1, P, P), (2, HD, D)]
        NU = len(OUT) * B

        @block.sync
        def _(sp):
            w = d["L1_attn_c_attn_w"]
            for j in range(2):
                sp.dma_start(ca[:, j, :], w[j * P:(j + 1) * P, :]).then_inc(ld, 16)
            sp.dma_start(ca[0:2 * HD, 2, :], w[D:NO, :]).then_inc(ld, 16)
            sp.dma_start(cp[:, :, :], d["L1_attn_c_proj_w"].rearrange("(k p) n -> p k n", p=P)).then_inc(ld, 16)
            cb = d["L1_attn_c_attn_b"]
            for j in range(2):
                sp.dma_start(qb[:, j:j + 1], bass.AP(tensor=cb.tensor, offset=j * P, ap=[[1, P], [1, 1]])).then_inc(ld, 16)
            sp.dma_start(kb_[:, :], bass.AP(tensor=cb.tensor, offset=D, ap=[[1, HD], [1, 1]])).then_inc(ld, 16)
            sp.dma_start(vb[:, :], rows_bcast(cb, D + HD, HD)).then_inc(ld, 16)
            sp.dma_start(g.cpb[:, :], rows_bcast(d["L1_attn_c_proj_b"], 0, D)).then_inc(ld, 16)
            sp.wait_ge(p3_ok, NU)
            for p in range(NPART):
                sp.dma_start(g.parts_d[p, 0:2].rearrange("x p n -> p x n"), part[p][:, 0:2, :]).then_inc(st, 16)
                sp.dma_start(g.parts_d[p, 2, 0:HD, :], part[p][0:HD, 2, :]).then_inc(st, 16)
            sp.wait_ge(st, 32 * NPART)

        @block.tensor
        def _(pe):
            pe.wait_ge(ld, 16 * 9)
            for j in range(5):
                if j >= 2:
                    pe.wait_ge(w_sb, j - 1)
                n = P if j != 2 else 2 * HD
                for k in range(KD):
                    src = ca[0:n, j, k * P:(k + 1) * P] if j < 3 else cp[:, j - 3, k * P:(k + 1) * P]
                    last = nc.tensor.transpose(ps[:, j % 2, k * P:k * P + n], src, g.idf[0:n, 0:n])
                last.then_inc(w_ps, 1)
            for c in range(NT):
                if c >= 2:
                    pe.wait_ge(t_sb, c - 1)
                for k in range(KD):
                    last = nc.tensor.transpose(ps[:, 2 + c % 2, k * P:(k + 1) * P], g.X[:, c, k * P:(k + 1) * P], g.idf[:, :])
                last.then_inc(t_ps, 1)
            pe.wait_ge(t_sb, NT)
            pe.wait_ge(w_sb, 5)
            for b in range(B):
                for t in range(4):
                    i = 4 * b + t
                    for k in range(KD):
                        last = nc.tensor.matmul(ps[:, 6, i * HD:(i + 1) * HD], xT[:, k, b, t * P:(t + 1) * P], caT[:, k, D + HD:NO], start=(k == 0), stop=(k == KD - 1))
            last.then_inc(v_ps, 1)
            for u in range(NU):
                x, n, c0 = OUT[u // B]
                b = u % B
                if u >= 2:
                    pe.wait_ge(r_ok, u - 1)
                for k in range(KD):
                    last = nc.tensor.matmul(ps[0:n, 4 + u % 2, :], caT[:, k, c0:c0 + n], xT[:, k, b, :], start=(k == 0), stop=(k == KD - 1))
                last.then_inc(q_ps, 1)

        @block.scalar
        def _(act):
            for j in range(5):
                act.wait_ge(w_ps, j + 1)
                n = P if j != 2 else 2 * HD
                dst = caT[:, :, j * P:j * P + n] if j < 3 else g.cpT[:, :, (j - 3) * P:(j - 2) * P]
                nc.scalar.copy(dst, ps[:, j % 2, 0:KD * P].rearrange("p (k m) -> p k m", k=KD)[:, :, 0:n]).then_inc(w_sb, 1)
            for c in range(NT):
                act.wait_ge(t_ps, c + 1)
                nc.scalar.copy(xT[:, :, :, c * R:(c + 1) * R], ps[:, 2 + c % 2, 0:KD * P].rearrange("p (k b i) -> p k b i", k=KD, b=B)).then_inc(t_sb, 1)
            for u in range(NU):
                x, n, c0 = OUT[u // B]
                b = u % B
                act.wait_ge(q_ps, u + 1)
                bias = qb[:, x:x + 1] if x < 2 else kb_[:, 0:1]
                nc.scalar.activation(part[0][0:n, x, b * N:(b + 1) * N], ps[0:n, 4 + u % 2, :], ACT.Identity, bias=bias).then_inc(p1_ok, 1)

        @block.vector
        def _(dve):
            nc.vector.memset(g.VA1[:, :, :], 1.0).then_inc(one, 1)
            dve.wait_ge(one, 1)
            dve.wait_ge(v_ps, 1)
            nc.vector.tensor_tensor(g.VA1[:, :, 0:HD], ps[:, 6, 0:16 * HD].rearrange("p (t e) -> p t e", e=HD), bcast(vb[:, :], [[0, 16], [1, HD]]), ALU.add).then_inc(v_ok, 1)
            for u in range(NU):
                x, n, c0 = OUT[u // B]
                b = u % B
                dve.wait_ge(p1_ok, u + 1)
                if u >= 2:
                    dve.wait_ge(p3_ok, u - 1)
                bias = qb[:, x:x + 1] if x < 2 else kb_[:, 0:1]
                nc.vector.scalar_tensor_tensor(out=rem[0:n, u % 2, :], in0=ps[0:n, 4 + u % 2, :], scalar=bias, in1=part[0][0:n, x, b * N:(b + 1) * N],
                                               op0=ALU.add, op1=ALU.subtract).then_inc(r_ok, 1)

        @block.gpsimd
        def _(pool):
            for u in range(NU):
                x, n, c0 = OUT[u // B]
                bs = slice((u % B) * N, (u % B + 1) * N)
                pool.wait_ge(r_ok, u + 1)
                nc.gpsimd.tensor_copy(part[1][0:n, x, bs], rem[0:n, u % 2, :]).then_inc(p2_ok, 1)
                pool.wait_ge(p2_ok, u + 1)
                nc.gpsimd.tensor_tensor(part[2][0:n, x, bs], rem[0:n, u % 2, :], part[1][0:n, x, bs], ALU.subtract).then_inc(p3_ok, 1)


def phase_moe(nc, g):
    with ExitStack() as ctx:
        sb = lambda n, s, d=F32: ctx.enter_context(nc.sbuf_tensor(f"moe_{n}", s, d))
        sem = semaphores(nc, ctx, f"moe_")
        ps = g.ps
        We, Wg, be = sb("experts", [P, KD, E, D]), sb("gate", [P, KD, E]), sb("bias", [E, D])
        xT = sb("xT", [P, 2, KD, P])
        lg, pr, mxl, rk, sm, cb = (sb("logits", [P, 2, E]), sb("exps", [P, 2, E]), sb("neg_max", [P, 2, 1]), sb("rank", [P, 2, E]), sb("sum", [P, 2, 2]),
                                   sb("combine", [P, 2, E]))
        cT = sb("combineT", [E, 2, P])
        order = sb("order", [P, E])
        acc = sb("acc", [P, 2, D])
        ld, or_ok, t_ps, t_sb, l_ps, gt, ex_ok, cb_ok, ct_ps, ct_sb, b_ps, y_ps, a_ok = (
            sem("loaded"), sem("order_ok"), sem("xT_psum"), sem("xT_sbuf"), sem("logits_psum"), sem("gate_steps"), sem("exps_ok"), sem("combine_ok"),
            sem("combineT_psum"), sem("combineT_sbuf"), sem("bias_psum"), sem("expert_psum"), sem("accumulated"))
        st = g.out_stored
        ln = LayerNorm(nc, ctx, "moeln", g.mhalf)
        block = ctx.enter_context(nc.Block())
        d = g.d
        GS = 6
        NA = E + 1

        @block.sync
        def _(sp):
            sp.dma_start(Wg[:, :, :], d["L1_ffn_Wg"].rearrange("(k p) n -> p k n", p=P)).then_inc(ld, 16)
            sp.dma_start(be[:, :], d["L1_ffn_b"]).then_inc(ld, 16)
            for e in range(E):
                sp.dma_start(We[:, :, e, :], d["L1_ffn_W"][e].rearrange("(k p) n -> p k n", p=P)).then_inc(ld, 16)
            for c in range(NT):
                sp.wait_ge(ln.y_ok, c + 1)
                for b in range(B):
                    sp.dma_start(g.out[b, c * R:(c + 1) * R, :], g.X[R * b:R * b + R, c, :]).then_inc(st, 16)
            sp.wait_ge(st, 16 * B * NT)

        @block.tensor
        def _(pe):
            pe.wait_ge(ld, 160)

            def gate(c):
                if c >= 2:
                    pe.wait_ge(t_sb, c - 1)
                for k in range(KD):
                    last = nc.tensor.transpose(ps[:, 0, k * P:(k + 1) * P], g.X[:, c, k * P:(k + 1) * P], g.idf[:, :])
                last.then_inc(t_ps, 1)
                pe.wait_ge(t_sb, c + 1)
                if c:
                    pe.wait_ge(gt, GS * (c - 1) + 1)
                for k in range(KD):
                    last = nc.tensor.matmul(ps[:, 1, 0:E], xT[:, c % 2, k, :], Wg[:, k, :], start=(k == 0), stop=(k == KD - 1))
                last.then_inc(l_ps, 1)

            def biases(c):
                pe.wait_ge(cb_ok, c + 1)
                if c:
                    pe.wait_ge(ct_sb, c)
                    pe.wait_ge(a_ok, NA * (c - 1) + 1)
                nc.tensor.transpose(ps[0:E, 2, 0:P], cb[:, c % 2, :], g.idf[:, :]).then_inc(ct_ps, 1)
                pe.wait_ge(ct_sb, c + 1)
                nc.tensor.matmul(ps[:, 3, 0:D], cT[:, c % 2, :], be[:, :], start=True, stop=True).then_inc(b_ps, 1)

            def experts(c):
                for e2 in range(E // 2):
                    n = c * (E // 2) + e2
                    if n >= 4:
                        m, r = (n - 4) // (E // 2), (n - 4) % (E // 2)
                        pe.wait_ge(a_ok, NA * m + 1 + 2 * (r + 1))
                    for k in range(KD):
                        last = nc.tensor.matmul(ps[:, 4 + n % 4, :], xT[:, c % 2, k, :], We[:, k, 2 * e2:2 * e2 + 2, :].rearrange("p e n -> p (e n)"),
                                                start=(k == 0), stop=(k == KD - 1))
                    last.then_inc(y_ps, 1)

            gate(0)
            for c in range(NT):
                experts(c)
                biases(c)
                if c + 1 < NT:
                    gate(c + 1)

        @block.scalar
        def _(act):
            def xT_out(c):
                act.wait_ge(t_ps, c + 1)
                if c >= 2:
                    act.wait_ge(y_ps, (c - 1) * (E // 2))
                nc.scalar.copy(xT[:, c % 2, :, :], ps[:, 0, 0:KD * P].rearrange("p (k m) -> p k m", k=KD)).then_inc(t_sb, 1)

            for c in range(NT):
                xT_out(c)
                act.wait_ge(gt, GS * c + 2)
                nc.scalar.activation(pr[:, c % 2, :], lg[:, c % 2, :], ACT.Exp, bias=mxl[:, c % 2, :], accum_out=sm[:, c % 2, 0:1]).then_inc(ex_ok, 1)
                act.wait_ge(ct_ps, c + 1)
                nc.scalar.copy(cT[:, c % 2, :], ps[0:E, 2, 0:P]).then_inc(ct_sb, 1)

        @block.gpsimd
        def _(pool):
            for e in range(E):
                nc.gpsimd.memset(order[:, e:e + 1], float(E - e)).then_inc(or_ok, 1)
            for c in range(NT):
                ln.rstd(pool, c)

        @block.vector
        def _(dve):
            def gate(c):
                s = c % 2
                if c == 0:
                    dve.wait_ge(or_ok, E)
                dve.wait_ge(l_ps, c + 1)
                nc.vector.tensor_copy(lg[:, s, :], ps[:, 1, 0:E]).then_inc(gt, 1)
                dve.wait_ge(gt, GS * c + 1)
                nc.vector.tensor_reduce(mxl[:, s, :], lg[:, s, :], AX.X, ALU.max, negate=True).then_inc(gt, 1)
                dve.wait_ge(gt, GS * c + 2)
                nc.vector.tensor_scalar(rk[:, s, :], lg[:, s, :], mxl[:, s, :], 0.0, ALU.add, ALU.is_equal).then_inc(gt, 1)
                dve.wait_ge(gt, GS * c + 3)
                nc.vector.tensor_tensor(rk[:, s, :], rk[:, s, :], order[:, :], ALU.mult).then_inc(gt, 1)
                dve.wait_ge(gt, GS * c + 4)
                nc.vector.tensor_reduce(sm[:, s, 1:2], rk[:, s, :], AX.X, ALU.max).then_inc(gt, 1)
                dve.wait_ge(ex_ok, c + 1)
                nc.vector.reciprocal(sm[:, s, 0:1], sm[:, s, 0:1]).then_inc(gt, 1)
                dve.wait_ge(gt, GS * c + 6)
                if c >= 2:
                    dve.wait_ge(ct_ps, c - 1)
                nc.vector.tensor_scalar(cb[:, s, :], rk[:, s, :], sm[:, s, 1:2], sm[:, s, 0:1], ALU.is_equal, ALU.mult).then_inc(cb_ok, 1)

            def add(c):
                s = c % 2
                dve.wait_ge(b_ps, c + 1)
                if c >= 2:
                    dve.wait_ge(ln.y_ok, c - 1)
                nc.vector.tensor_tensor(acc[:, s, :], g.X[:, c, :], ps[:, 3, 0:D], ALU.add).then_inc(a_ok, 1)
                for e in range(E):
                    if e % 2 == 0:
                        dve.wait_ge(y_ps, c * (E // 2) + e // 2 + 1)
                    dve.wait_ge(a_ok, NA * c + e + 1)
                    nc.vector.scalar_tensor_tensor(out=acc[:, s, :], in0=ps[:, 4 + (c * (E // 2) + e // 2) % 4, (e % 2) * D:(e % 2 + 1) * D], scalar=cb[:, s, e:e + 1],
                                                   in1=acc[:, s, :], op0=ALU.mult, op1=ALU.add).then_inc(a_ok, 1)
                dve.wait_ge(a_ok, NA * (c + 1))
                ln.stats(dve, c, acc[:, s, :])

            for c in range(NT):
                gate(c)
                add(c)
                if c:
                    ln.apply(dve, c - 1, g.X[:, c - 1, :], acc[:, (c - 1) % 2, :])
            ln.apply(dve, NT - 1, g.X[:, NT - 1, :], acc[:, (NT - 1) % 2, :])


def program(nc, g, upto=99):
    with ExitStack() as ctx:
        sb = lambda n, s, d=F32: ctx.enter_context(nc.sbuf_tensor(n, s, d))
        g.ps = ctx.enter_context(nc.psum_tensor("psum", [P, 8, 512], F32))
        g.out_stored = ctx.enter_context(nc.semaphore("output_stored"))
        g.X = sb("x_rows", [P, NT, D])
        g.idf, g.idb = sb("identity", [P, P]), sb("identity_bf16", [P, P], BF16)
        g.maskq, g.maskk = sb("mask_q_rows", [P, P], BF16), sb("mask_k_rows", [P, P], BF16)
        g.mhalf = sb("minus_half", [P, G4 * H])
        rows32k = sb("rows_32k", [P, NT * 2 * D])
        g.QKR = rows32k[:, :].rearrange("p (c n) -> p c n", c=NT)
        g.AT = rows32k[:, :].rearrange("p (c i h) -> p c i h", c=NT, i=R)
        g.VN = rows32k[:, :].rearrange("p (b k n) -> p b k n", b=B, k=4)
        with ExitStack() as c2:
            sb2 = lambda n, s, d=F32: c2.enter_context(nc.sbuf_tensor(n, s, d))
            g.V = sb2("v_rows", [P, NT, D])
            g.KB = sb2("kb_rows", [P, NT, D])
            g.KT = sb2("kT", [P, HG, B, N])
            g.beta = sb2("beta", [P, NT, H])
            phase_qkv(nc, g)
            if upto <= 1:
                return
            g.TT = sb2("invT", [P, NT, R, H])
            phase_delta(nc, g)
            if upto <= 2:
                return
        with ExitStack() as c2:
            OT = c2.enter_context(nc.sbuf_tensor("l0_heads_out", [P, HG, NT, P], F32))
            phase_attention(nc, g, "l0", OT, False, g.parts_d, 2 * P, lambda b, kb, h: g.VN[:, b, kb, 32 * h:32 * h + 32])
            Wo = c2.enter_context(nc.sbuf_tensor("l0_wo", [P, KD, D], F32))

            def load_wo(sp, s):
                if sp is not None:
                    sp.dma_start(Wo[:, :, :], g.Wo.rearrange("(k p) n -> p k n", p=P)).then_inc(s, 16)
                return Wo

            phase_out_proj(nc, g, "l0p", OT, load_wo, None)
            if upto <= 3:
                return
        with ExitStack() as c2:
            sb2 = lambda n, s, d=F32: c2.enter_context(nc.sbuf_tensor(n, s, d))
            g.Wap, g.bap = sb2("w_amp_phase", [P, KD, 2 * D]), sb2("b_amp_phase", [P, 2 * D])
            g.Wst, g.bst = sb2("w_stages", [P, 4, KD, D]), sb2("b_stages", [P, 4, D])
            g.gam, g.bet = sb2("ln_gamma", [P, 4, D]), sb2("ln_beta", [P, 4, D])
            phase_weights(nc, g)
            phase_ffn(nc, g)
            if upto <= 4:
                return
        with ExitStack() as c2:
            sb2 = lambda n, s, d=F32: c2.enter_context(nc.sbuf_tensor(n, s, d))
            OT = sb2("l1_heads_out", [P, HG, NT, P])
            g.cpT, g.cpb, g.VA1 = sb2("c_projT", [P, KD, D]), sb2("c_proj_b", [P, D]), sb2("v1_rows", [P, B * 4, 2 * HD])
            phase_l1_qkv(nc, g)
            phase_attention(nc, g, "l1", OT, True, g.parts_d, 2 * P, lambda b, kb, h: g.VA1[:, 4 * b + kb, :])

            def load_cp(sp, s):
                if sp is not None:
                    sp.sem_inc(s, 16)
                return g.cpT

            phase_out_proj(nc, g, "l1p", OT, load_cp, g.cpb)
            if upto <= 5:
                return
        phase_moe(nc, g)


def consts():
    low = np.float32(-3e38)
    q, k = np.arange(P)[:, None], np.arange(P)[None, :]
    inv = (1.0 / (np.float32(10000.0) ** (np.arange(0, HD, 2, dtype=np.float32) / np.float32(HD)))).astype(np.float32)
    th = (np.arange(N, dtype=np.float32)[:, None] * inv).astype(np.float32)
    cos, sin = np.cos(th), np.sin(th)
    lay = lambda a: np.ascontiguousarray(np.tile(a.reshape(NT, R, HD).transpose(1, 0, 2), (B, 1, 1)), dtype=np.float32)
    return {
        "ident": np.eye(P, dtype=np.float32),
        "maskq": np.where(k > q, low, np.float32(0)),
        "maskk": np.where(k < q, low, np.float32(0)),
        "cos": lay(np.concatenate([cos, cos], 1)), "sin": lay(np.concatenate([-sin, sin], 1)),
    }


_INS = ["L0_attn_x", "L0_attn_Wq", "L0_attn_Wk", "L0_attn_Wv", "L0_attn_Wo", "L0_attn_Wb", "L0_ffn_amp_w", "L0_ffn_amp_b",
        "L0_ffn_ph_w", "L0_ffn_ph_b", "L0_ffn_ent_w", "L0_ffn_ent_b", "L0_ffn_ent_pw", "L0_ffn_ent_pb", "L0_ffn_path_w",
        "L0_ffn_path_b", "L0_ffn_phase", "L0_ffn_ln3_g", "L0_ffn_ln3_b", "L0_ffn_ln4_g", "L0_ffn_ln4_b",
        "L1_attn_c_attn_w", "L1_attn_c_attn_b", "L1_attn_c_proj_w", "L1_attn_c_proj_b", "L1_ffn_Wg", "L1_ffn_W", "L1_ffn_b"]


def build(nc, arrays, upto=99):
    g = Ctx()
    d = {n: nc.dram_tensor(f"in_{n}_dram", a.shape, mybir.dt.from_np(a.dtype), kind="ExternalInput").ap() for n, a in arrays.items()}
    g.x_in, g.Wq, g.Wk, g.Wv, g.Wo, g.Wb = (d[n] for n in _INS[:6])
    g.d = d
    g.ident_d, g.maskq_d, g.maskk_d, g.cos_d, g.sin_d = (d[n] for n in ("ident", "maskq", "maskk", "cos", "sin"))
    g.out = nc.dram_tensor("out_0_dram", (B, N, D), F32, kind="ExternalOutput").ap()
    scratch = lambda n, s, t: nc.dram_tensor(n, s, t, kind="Internal").ap()
    g.parts_d = scratch("parts_scratch", (NPART, 4, P, B * N), BF16)
    g.gram_d = scratch("gram_scratch", (P, NT * 2 * H * CH), F32)
    g.inv_d = scratch("inverse_scratch", (2, P, CH * H * CH), F32)
    program(nc, g, upto)


def kernel(**inputs):
    import concourse.bacc as _bacc
    from concourse.bass_utils import run_bass_kernel_spmd as _run

    nc = _bacc.Bacc("TRN2", target_bir_lowering=False, num_devices=1)
    arrays = {n: np.ascontiguousarray(inputs[n]) for n in _INS}
    arrays.update(consts())
    build(nc, arrays)
    r = _run(nc, [{f"in_{n}_dram": a for n, a in arrays.items()}], core_ids=[0])
    return r.results[0]["out_0_dram"]
```

```python
from contextlib import ExitStack

import numpy as np

import concourse.bass as bass
from concourse import mybir

ALU = mybir.AluOpType
ACT = mybir.ActivationFunctionType
AX = mybir.AxisListType
F32 = mybir.dt.float32
BF16 = mybir.dt.bfloat16

P = 128
B, N, D, H = 4, 512, 256, 16
HD = D // H
KD = D // P
R = 32
NT = N // R
G4 = 4
NG = NT // G4
HG = H // 4
CH = 16
EPS_L2, EPS_LN = 1e-6, 1e-5
SCALE = HD ** -0.5
NPART = 3
PAIRS = [(0, 0), (0, 1), (1, 0), (1, 1), (0, 2), (2, 0)]
KR = 16 * len(PAIRS)
KRM = KR + NPART
E = 8
PI = float(np.pi)


class Ctx:
    pass


def semaphores(nc, ctx, prefix):
    held = []
    ctx.callback(lambda: (nc.clear_and_free_semaphores(held), nc.all_engine_barrier()))

    def sem(name):
        held.append(nc.alloc_semaphore(prefix + name))
        return held[-1]

    return sem


def bcast(ap, dims):
    return bass.AP(tensor=ap.tensor, offset=ap.offset, ap=[list(ap.ap[0])] + [list(d) for d in dims])


def rows_bcast(dram, offset, n):
    return bass.AP(tensor=dram.tensor, offset=dram.offset + offset, ap=[[0, P], [1, n]])


def phase_qkv(nc, g):
    with ExitStack() as ctx:
        sb = lambda n, s, d=F32: ctx.enter_context(nc.sbuf_tensor(n, s, d))
        sem = semaphores(nc, ctx, "")
        WC = 3 * D + H
        w = sb("l0_wqkvb", [P, KD, WC])
        xT = sb("l0_xT", [P, G4, KD, P])
        qk = g.QKR
        kn = sb("l0_kn_rows", [P, G4, H, 32])
        t1 = sb("rope_t1", [P, G4, 2 * D])
        t2 = sb("rope_t2", [P, G4, 2 * D])
        rem = sb("split_rem", [P, 2, 4, P])
        masks = rem[:, 0, 0:2, :]
        part = [sb(f"qk_part{p}", [P, 4, B, N], BF16) for p in range(NPART)]
        cosT, sinT = sb("rope_cos", [P, NT, HD]), sb("rope_sin", [P, NT, HD])
        ksq = sb("k_squares", [P, G4, D])
        ss = sb("k_sumsq", [P, G4, H])
        ld_x, ld_w, ld_c = sem("x_loaded"), sem("w_loaded"), sem("consts_loaded")
        xT_ps, xT_sb = sem("xT_in_psum"), sem("xT_in_sbuf")
        qk_ps, v_ps, qk_sb, v_sb = sem("qk_in_psum"), sem("v_in_psum"), sem("qk_in_sbuf"), sem("v_in_sbuf")
        bexp, beta_ok = sem("beta_exp"), sem("beta_steps")
        pad_ok, cos_ok, sin_ok, rot_ok = sem("kn_pad_zeroed"), sem("cos_product"), sem("sin_product"), sem("rotated")
        sq_ok, ss_ok, rs_ok, kn_ok, kb_ok = sem("k_squared"), sem("k_sums"), sem("k_rsqrt"), sem("kn_rows"), sem("kb_rows")
        kt_ps, qt_ps, kt_sb, p1_ok, r1_ok, p2_ok, p3_ok = (sem("knT_psum"), sem("qkT_psum"), sem("knT_sbuf"), sem("part1"),
                                                         sem("remainder1"), sem("part2"), sem("part3"))
        st, cbf = sem("parts_stored"), sem("bf16_consts")
        ps = g.ps
        x_d = g.x_in
        block = ctx.enter_context(nc.Block())

        @block.sync
        def _(sp):
            for b in range(B):
                sp.dma_start(g.X[R * b:R * b + R, :, :], x_d[b].rearrange("(c i) d -> i c d", i=R)).then_inc(ld_x, 16)
            sp.dma_start(g.idf[:, :], g.ident_d).then_inc(ld_c, 16)
            sp.dma_start(masks[:, 0, :], g.maskq_d).then_inc(ld_c, 16)
            sp.dma_start(masks[:, 1, :], g.maskk_d).then_inc(ld_c, 16)
            sp.dma_start(cosT[:, :, :], g.cos_d).then_inc(ld_c, 16)
            sp.dma_start(sinT[:, :, :], g.sin_d).then_inc(ld_c, 16)
            sp.wait_ge(p3_ok, NT)
            for p in range(NPART):
                sp.dma_start(g.parts_d[p].rearrange("x p n -> p x n"),
                             part[p][:, :, :, :].rearrange("p x b n -> p x (b n)")).then_inc(st, 16)
            sp.wait_ge(st, 16 * NPART)

        @block.scalar
        def _(act):
            for j, wd in enumerate((g.Wq, g.Wk, g.Wv)):
                act.dma_start(w[:, :, j * D:(j + 1) * D], wd.rearrange("(k p) n -> p k n", p=P)).then_inc(ld_w, 16)
            act.dma_start(w[:, :, 3 * D:], g.Wb.rearrange("(k p) n -> p k n", p=P)).then_inc(ld_w, 16)

            def transposed(c):
                act.wait_ge(xT_ps, c + 1)
                if c >= G4:
                    act.wait_ge(v_ps, c - G4 + 1)
                nc.scalar.copy(xT[:, c % G4, :, :], ps[:, c % 2, 0:KD * P].rearrange("p (k m) -> p k m", k=KD)).then_inc(xT_sb, 1)

            def rows(c):
                act.wait_ge(qk_ps, c + 1)
                nc.scalar.copy(qk[:, c, :], ps[:, 2 + c % 2, :]).then_inc(qk_sb, 1)

            def operands(c):
                act.wait_ge(kt_ps, c + 1)
                nc.scalar.copy(g.KT[:, :, :, c * R:(c + 1) * R],
                               ps[:, 6, :].rearrange("p (g b i) -> p g b i", g=HG, b=B)).then_inc(kt_sb, 1)
                act.wait_ge(qt_ps, c + 1)
                nc.scalar.copy(part[0][:, :, :, c * R:(c + 1) * R],
                               ps[:, 7, :].rearrange("p (x b i) -> p x b i", x=4, b=B)).then_inc(p1_ok, 1)

            def second_part(c):
                act.wait_ge(r1_ok, c + 1)
                nc.scalar.copy(part[1][:, :, :, c * R:(c + 1) * R], rem[:, c % 2, :, :].rearrange("p x (b i) -> p x b i", b=B)).then_inc(p2_ok, 1)

            for q in range(NG + 1):
                for j in range(G4):
                    if q < NG:
                        transposed(q * G4 + j)
                        rows(q * G4 + j)
                if q < NG:
                    act.wait_ge(v_sb, (q + 1) * G4)
                    gs = slice(q * G4, (q + 1) * G4)
                    nc.scalar.activation(g.beta[:, gs, :], g.beta[:, gs, :], ACT.Exp, scale=-1.0).then_inc(bexp, 1)
                if q >= 1:
                    for j in range(G4):
                        operands((q - 1) * G4 + j)
                        if j:
                            second_part((q - 1) * G4 + j - 1)
                    second_part(q * G4 - 1)
                if q < NG:
                    act.wait_ge(ss_ok, q + 1)
                    act.wait_ge(pad_ok, 3)
                    nc.scalar.activation(ss[:, :, :], ss[:, :, :], ACT.Sqrt, bias=g.eps[:, 1:2]).then_inc(rs_ok, 1)

        @block.vector
        def _(dve):
            nc.vector.memset(g.eps[:, 0:1], EPS_LN).then_inc(pad_ok, 1)
            nc.vector.memset(g.eps[:, 1:2], EPS_L2).then_inc(pad_ok, 1)
            nc.vector.memset(kn[:, :, :, :], 0.0).then_inc(pad_ok, 1)

            def evac(c):
                dve.wait_ge(v_ps, c + 1)
                nc.vector.tensor_copy(g.V[:, c, :], ps[:, 4 + c % 2, 0:D])
                nc.vector.tensor_copy(g.beta[:, c, :], ps[:, 4 + c % 2, D:D + H]).then_inc(v_sb, 1)

            def group(q):
                gs = slice(q * G4, (q + 1) * G4)
                be = g.beta[:, gs, :]
                dve.wait_ge(bexp, q + 1)
                nc.vector.tensor_scalar(be, be, 0.5, 0.5, ALU.mult, ALU.add).then_inc(beta_ok, 1)
                dve.wait_ge(qk_sb, (q + 1) * G4)
                if q == 0:
                    dve.wait_ge(ld_c, 80)
                else:
                    dve.wait_ge(rot_ok, q)
                t1v = t1[:, :, :].rearrange("p c (h e) -> p c h e", e=HD)
                qv = qk[:, gs, :].rearrange("p c (h e) -> p c h e", e=HD)
                cv = bcast(cosT[:, gs, :], [[HD, G4], [0, 2 * H], [1, HD]])
                nc.vector.tensor_tensor(t1v, qv, cv, ALU.mult).then_inc(cos_ok, 1)
                dve.wait_ge(beta_ok, 2 * q + 1)
                nc.vector.reciprocal(be, be).then_inc(beta_ok, 1)
                dve.wait_ge(sq_ok, q + 1)
                if q:
                    dve.wait_ge(kn_ok, q)
                nc.vector.tensor_reduce(ss[:, :, :], ksq[:, :, :].rearrange("p c (h e) -> p c h e", e=HD), AX.X, ALU.add).then_inc(ss_ok, 1)
                dve.wait_ge(sin_ok, 2 * (q + 1))
                dve.wait_ge(cos_ok, q + 1)
                nc.vector.tensor_tensor(qk[:, gs, :], t1[:, :, :], t2[:, :, :], ALU.add).then_inc(rot_ok, 1)
                dve.wait_ge(rs_ok, 2 * q + 1)
                nc.vector.reciprocal(ss[:, :, :], ss[:, :, :]).then_inc(rs_ok, 1)

            def remainder(c):
                dve.wait_ge(p1_ok, c + 1)
                if c == 0:
                    dve.wait_ge(cbf, 3)
                if c >= 2:
                    dve.wait_ge(p3_ok, c - 1)
                nc.vector.tensor_tensor(rem[:, c % 2, :, :].rearrange("p x (b i) -> p x b i", b=B),
                                        ps[:, 7, :].rearrange("p (x b i) -> p x b i", x=4, b=B),
                                        part[0][:, :, :, c * R:(c + 1) * R], ALU.subtract).then_inc(r1_ok, 1)

            for q in range(NG + 1):
                if q < NG:
                    for j in range(G4):
                        evac(q * G4 + j)
                if q >= 1:
                    for j in range(G4):
                        remainder((q - 1) * G4 + j)
                if q < NG:
                    group(q)

        @block.gpsimd
        def _(pool):
            def group(q):
                gs = slice(q * G4, (q + 1) * G4)
                qv = qk[:, gs, :].rearrange("p c (h e) -> p c h e", e=HD)
                t2v = t2[:, :, :].rearrange("p c (h e) -> p c h e", e=HD)
                pool.wait_ge(qk_sb, (q + 1) * G4)
                if q == 0:
                    pool.wait_ge(ld_c, 80)
                else:
                    pool.wait_ge(rot_ok, q)
                if q >= 1:
                    pool.wait_ge(ss_ok, q)
                nc.gpsimd.tensor_tensor(ksq[:, :, :], qk[:, gs, D:], qk[:, gs, D:], ALU.mult).then_inc(sq_ok, 1)
                for lo, hi in ((0, 8), (8, 0)):
                    sv = bcast(sinT[:, gs, lo:lo + 8], [[HD, G4], [0, 2 * H], [1, 8]])
                    nc.gpsimd.tensor_tensor(t2v[:, :, :, lo:lo + 8], qv[:, :, :, hi:hi + 8], sv, ALU.mult).then_inc(sin_ok, 1)
                pool.wait_ge(rs_ok, 2 * q + 2)
                pool.wait_ge(rot_ok, q + 1)
                if q >= 1:
                    pool.wait_ge(kt_ps, q * G4)
                kv = qk[:, gs, D:].rearrange("p c (h e) -> p c h e", e=HD)
                nc.gpsimd.tensor_tensor(kn[:, :, :, 0:HD], kv, bcast(ss[:, :, :], [[H, G4], [1, H], [0, HD]]), ALU.mult).then_inc(kn_ok, 1)
                pool.wait_ge(kn_ok, q + 1)
                pool.wait_ge(beta_ok, 2 * q + 2)
                nc.gpsimd.tensor_tensor(g.KB[:, gs, :].rearrange("p c (h e) -> p c h e", e=HD), kn[:, :, :, 0:HD],
                                        bcast(g.beta[:, gs, :], [[H, G4], [1, H], [0, HD]]), ALU.mult).then_inc(kb_ok, 1)

            pool.wait_ge(ld_c, 80)
            for dst, src in ((g.idb, g.idf[:, :]), (g.maskq, masks[:, 0, :]), (g.maskk, masks[:, 1, :])):
                nc.gpsimd.tensor_copy(dst[:, :], src).then_inc(cbf, 1)

            def split(c):
                pool.wait_ge(r1_ok, c + 1)
                r = rem[:, c % 2, :, :].rearrange("p x (b i) -> p x b i", b=B)
                cs = slice(c * R, (c + 1) * R)
                pool.wait_ge(p2_ok, c + 1)
                nc.gpsimd.tensor_tensor(part[2][:, :, :, cs], r, part[1][:, :, :, cs], ALU.subtract).then_inc(p3_ok, 1)

            for q in range(NG + 1):
                if q >= 1:
                    for j in range(G4):
                        split((q - 1) * G4 + j)
                if q < NG:
                    group(q)

        @block.tensor
        def _(pe):
            pe.wait_ge(ld_x, 64)
            pe.wait_ge(ld_c, 80)

            def xpose(c):
                if c >= 2:
                    pe.wait_ge(xT_sb, c - 1)
                for k in range(KD):
                    last = nc.tensor.transpose(ps[:, c % 2, k * P:(k + 1) * P], g.X[:, c, k * P:(k + 1) * P], g.idf[:, :])
                last.then_inc(xT_ps, 1)

            def project(c):
                pe.wait_ge(xT_sb, c + 1)
                if c == 0:
                    pe.wait_ge(ld_w, 64)
                if c >= 2:
                    pe.wait_ge(qk_sb, c - 1)
                    pe.wait_ge(v_sb, c - 1)
                for k in range(KD):
                    last = nc.tensor.matmul(ps[:, 2 + c % 2, :], xT[:, c % G4, k, :], w[:, k, 0:2 * D], start=(k == 0), stop=(k == KD - 1))
                last.then_inc(qk_ps, 1)
                for k in range(KD):
                    last = nc.tensor.matmul(ps[:, 4 + c % 2, 0:D + H], xT[:, c % G4, k, :], w[:, k, 2 * D:], start=(k == 0), stop=(k == KD - 1))
                last.then_inc(v_ps, 1)

            def operands(c):
                q, j = c // G4, c % G4
                pe.wait_ge(kn_ok, q + 1)
                if c >= 1:
                    pe.wait_ge(kt_sb, c)
                for x in range(HG):
                    last = nc.tensor.transpose(ps[:, 6, x * P:(x + 1) * P], kn[:, j, 4 * x:4 * x + 4, :].rearrange("p h e -> p (h e)"), g.idf[:, :])
                last.then_inc(kt_ps, 1)
                pe.wait_ge(kb_ok, q + 1)
                pe.wait_ge(rot_ok, q + 1)
                if c >= 1:
                    pe.wait_ge(r1_ok, c)
                for x in range(KD):
                    nc.tensor.transpose(ps[:, 7, x * P:(x + 1) * P], qk[:, c, x * P:(x + 1) * P], g.idf[:, :])
                for x in range(KD):
                    last = nc.tensor.transpose(ps[:, 7, (2 + x) * P:(3 + x) * P], g.KB[:, c, x * P:(x + 1) * P], g.idf[:, :])
                last.then_inc(qt_ps, 1)

            xpose(0)
            for c in range(NT):
                if c + 1 < NT:
                    xpose(c + 1)
                project(c)
                if c % G4 == G4 - 1 and c >= G4:
                    for j in range(G4):
                        operands((c // G4 - 1) * G4 + j)
            for j in range(G4):
                operands((NG - 1) * G4 + j)


def phase_delta(nc, g):
    with ExitStack() as ctx:
        sem = semaphores(nc, ctx, "")
        ps = g.ps
        with ExitStack() as c1:
            sb = lambda n, s, d=F32: c1.enter_context(nc.sbuf_tensor(n, s, d))
            AT = g.AT
            TT = g.TT
            TN = sb("inv_first", [P, NT, CH, H])
            L = sb("chunk_A", [P, CH, CH, H])
            T = sb("chunk_inv", [P, CH, CH, H])
            TC = L
            tmp = sb("update", [P, 64 * CH])
            Xs = sb("cross", [P, 2, H * CH])
            gram_ps, at_ok, at_dram, l_ok = sem("gram_psum"), sem("gram_rows"), sem("gram_stored"), sem("chunk_A_loaded")
            t_init, t_step, t_copy, t_dram, tt_ok, tt_zero = (sem("inv_init"), sem("inv_step"), sem("inv_copied"), sem("inv_stored"),
                                                              sem("inv_loaded"), sem("TT_zeroed"))
            psz, x_ps, x_sb, y_ps, y_sb = (sem("psum_zeroed"), sem("cross_psum"), sem("cross_sbuf"), sem("joined_psum"), sem("joined"))
            block = c1.enter_context(nc.Block())

            @block.tensor
            def _(pe):
                for c in range(NT):
                    if c >= 2:
                        pe.wait_ge(at_ok, 2 * (c - 1))
                    o = 4 * (c % 2)
                    for h in range(H):
                        gq, j = h // 4, h % 4
                        for b in range(B):
                            kt = g.KT[32 * j:32 * j + HD, gq, b, c * R:(c + 1) * R]
                            last = nc.tensor.matmul(ps[R * b:R * b + R, o + j, R * gq:R * gq + R], kt, kt, start=True, stop=True)
                    last.then_inc(gram_ps, 1)
                pe.wait_ge(psz, 1)
                pe.wait_ge(tt_ok, 16 * 12)
                pe.wait_ge(at_ok, 2 * NT)

                def cross(c):
                    if c >= 2:
                        pe.wait_ge(x_sb, c - 1)
                    for h in range(H):
                        for b in range(B):
                            a = AT[R * b:R * b + CH, c, :, h]
                            last = nc.tensor.matmul(ps[R * b:R * b + R, 4 + c % 2, h * CH:(h + 1) * CH], a,
                                                    TN[R * b:R * b + CH, c, :, h], start=True, stop=True)
                    last.then_inc(x_ps, 1)

                cross(0)
                for c in range(NT):
                    if c + 1 < NT:
                        cross(c + 1)
                    pe.wait_ge(x_sb, c + 1)
                    if c >= 2:
                        pe.wait_ge(y_sb, c - 1)
                    for h in range(H):
                        for b in range(B):
                            last = nc.tensor.matmul(ps[R * b:R * b + CH, 6 + c % 2, h * CH:(h + 1) * CH],
                                                    Xs[R * b:R * b + R, c % 2, h * CH:(h + 1) * CH],
                                                    TT[R * b:R * b + R, c, CH:R, h], start=True, stop=True)
                    last.then_inc(y_ps, 1)

            @block.vector
            def _(dve):
                for c in range(NT):
                    dve.wait_ge(gram_ps, c + 1)
                    o = 4 * (c % 2)
                    bt = g.beta[:, c, :]
                    for hf in range(2):
                        src = ps[:, o:o + 4, 0:P].rearrange("p j (q f i) -> p j q f i", q=HG, f=2)[:, :, :, hf, :]
                        dst = AT[:, c, CH * hf:CH * hf + CH, :].rearrange("p i (q j) -> p j q i", q=HG)
                        nc.vector.tensor_tensor(dst, src, bcast(bt, [[1, 4], [4, HG], [0, CH]]), ALU.mult).then_inc(at_ok, 1)
                dve.wait_ge(at_ok, 2 * NT)
                nc.vector.memset(ps[:, 6:8, :], 0.0).then_inc(psz, 1)
                dve.wait_ge(l_ok, 16 * 2 * B)
                dve.wait_ge(t_init, CH + 1)
                for j in range(CH - 1):
                    n_m, n_i = j + 1, CH - 1 - j
                    t = bcast(tmp[:, :], [[H * n_i, n_m], [H, n_i], [1, H]])
                    a = bcast(L[:, j, j + 1:, :], [[0, n_m], [H, n_i], [1, H]])
                    tj = bcast(T[:, 0:1, j:j + 1, :], [[H * CH, n_m], [0, n_i], [1, H]])
                    ti = T[:, 0:n_m, j + 1:, :]
                    if j:
                        dve.wait_ge(t_step, 2 * j)
                    nc.vector.tensor_tensor(t, a, tj, ALU.mult).then_inc(t_step, 1)
                    dve.wait_ge(t_step, 2 * j + 1)
                    nc.vector.tensor_tensor(ti, ti, t, ALU.subtract).then_inc(t_step, 1)
                for c in range(NT):
                    dve.wait_ge(y_ps, c + 1)
                    nc.vector.tensor_tensor(TT[:, c, CH:R, :], TT[:, c, CH:R, :], ps[:, 6 + c % 2, 0:H * CH].rearrange("p (h i) -> p i h", h=H),
                                            ALU.subtract).then_inc(y_sb, 1)

            @block.gpsimd
            def _(pool):
                nc.gpsimd.memset(T[:, :, :, :], 0.0).then_inc(t_init, 1)
                pool.wait_ge(t_init, 1)
                for m in range(CH):
                    nc.gpsimd.memset(T[:, m, m, :], 1.0).then_inc(t_init, 1)
                nc.gpsimd.memset(TT[:, :, :, :], 0.0).then_inc(tt_zero, 1)

            @block.scalar
            def _(act):
                act.wait_ge(t_step, 2 * (CH - 1))
                nc.scalar.copy(TC[:, :, :, :].rearrange("p i m h -> p m i h"), T[:, :, :, :]).then_inc(t_copy, 1)
                for c in range(NT):
                    act.wait_ge(x_ps, c + 1)
                    if c >= 2:
                        act.wait_ge(y_ps, c - 1)
                    nc.scalar.copy(Xs[:, c % 2, :], ps[:, 4 + c % 2, 0:H * CH]).then_inc(x_sb, 1)

            @block.sync
            def _(sp):
                W = H * CH
                for q in range(NG):
                    sp.wait_ge(at_ok, 2 * G4 * (q + 1))
                    o = G4 * 2 * W
                    sp.dma_start(g.gram_d[:, q * o:(q + 1) * o], AT[:, q * G4:(q + 1) * G4, :, :].rearrange("p c i h -> p (c i h)")).then_inc(at_dram, 16)
                sp.wait_ge(at_dram, 16 * NG)
                for b in range(B):
                    for hf in range(2):
                        src = bass.AP(tensor=g.gram_d.tensor, offset=((R * b + CH * hf) * NT * 2 + hf) * W,
                                      ap=[[2 * W, NT], [2 * NT * W, CH], [1, W]])
                        p0 = 2 * NT * b + hf
                        sp.dma_start(L[p0:p0 + 2 * NT - 1:2, :, :, :].rearrange("p j i h -> p j (i h)"), src).then_inc(l_ok, 16)
                sp.wait_ge(t_step, 2 * (CH - 1))
                sp.dma_start(g.inv_d[0], T[:, :, :, :].rearrange("p m i h -> p (m i h)")).then_inc(t_dram, 16)
                sp.wait_ge(t_copy, 1)
                sp.dma_start(g.inv_d[1], TC[:, :, :, :].rearrange("p i m h -> p (i m h)")).then_inc(t_dram, 16)
                sp.wait_ge(t_dram, 32)
                sp.wait_ge(tt_zero, 1)
                for b in range(B):
                    for hf in range(2):
                        src = bass.AP(tensor=g.inv_d.tensor, offset=(2 * NT * b + hf) * CH * W,
                                      ap=[[W, CH], [2 * CH * W, NT], [1, W]])
                        sp.dma_start(TT[R * b + CH * hf:R * b + CH * hf + CH, :, CH * hf:CH * hf + CH, :].rearrange("p c i h -> p c (i h)"), src).then_inc(tt_ok, 16)
                    src = bass.AP(tensor=g.inv_d.tensor, offset=P * CH * W + 2 * NT * b * CH * W,
                                  ap=[[W, CH], [2 * CH * W, NT], [1, W]])
                    sp.dma_start(TN[R * b:R * b + CH, :, :, :].rearrange("p c m h -> p c (m h)"), src).then_inc(tt_ok, 16)

        sb = lambda n, s, d=F32: ctx.enter_context(nc.sbuf_tensor(n, s, d))
        TT = g.TT
        S = sb("state", [P, B, HG, HD])
        rhs = sb("scan_rhs", [P, D])
        NV = 4
        VA = sb("v_new", [P, NV, H, 2 * HD])
        z_ok = sem("scan_zeroed")
        ks_ps, rhs_ok, vn_ps, vn_ok, su_ps, s_ok = ([sem(f"{n}{f}") for f in range(2)] for n in ("KS_psum", "rhs_rows", "v_new_psum", "v_new_rows",
                                                                                                 "state_psum", "state_ok"))
        va_out = [sem(f"v_new_stored{i}") for i in range(NV)]
        block = ctx.enter_context(nc.Block())

        HEADS = [[4 * gq + 2 * f + j for gq in range(HG) for j in range(2)] for f in range(2)]

        @block.tensor
        def _(pe):
            pe.wait_ge(z_ok, 3)
            for c in range(NT):
                if c:
                    for f in range(2):
                        pe.wait_ge(s_ok[f], c)
                        for h in HEADS[f]:
                            gq, j = h // 4, h % 4
                            for b in range(B):
                                last = nc.tensor.matmul(ps[R * b:R * b + R, j, HD * gq:HD * gq + HD], g.KT[32 * j:32 * j + HD, gq, b, c * R:(c + 1) * R],
                                                        S[32 * j:32 * j + HD, b, gq, :], start=True, stop=True)
                        last.then_inc(ks_ps[f], 1)
                for f in range(2):
                    pe.wait_ge(rhs_ok[f], c + 1)
                    for n, h in enumerate(HEADS[f]):
                        for b in range(B):
                            last = nc.tensor.matmul(ps[R * b:R * b + R, 2 * f, P + n * HD:P + (n + 1) * HD], TT[R * b:R * b + R, c, :, h],
                                                    rhs[R * b:R * b + R, h * HD:(h + 1) * HD], start=True, stop=True)
                    last.then_inc(vn_ps[f], 1)
                if c + 1 < NT:
                    for f in range(2):
                        pe.wait_ge(vn_ok[f], c + 1)
                        for b in range(B):
                            for h in HEADS[f]:
                                gq, j = h // 4, h % 4
                                last = nc.tensor.matmul(ps[32 * j:32 * j + HD, 4 + b, HD * gq:HD * gq + HD], g.KB[R * b:R * b + R, c, h * HD:(h + 1) * HD],
                                                        VA[R * b:R * b + R, c % NV, h, 0:HD], start=True, stop=True)
                        last.then_inc(su_ps[f], 1)

        @block.vector
        def _(dve):
            nc.vector.memset(ps[:, 4:8, 0:64], 0.0).then_inc(z_ok, 1)
            nc.vector.memset(S[:, :, :, :], 0.0).then_inc(z_ok, 1)
            nc.vector.memset(VA[:, :, :, :], 1.0).then_inc(z_ok, 1)
            dve.wait_ge(z_ok, 3)

            def half(ap, f):
                return ap.rearrange("p (q j e) -> p j q e", q=HG, j=4)[:, 2 * f:2 * f + 2, :, :]

            for c in range(NT):
                for f in range(2):
                    if c:
                        dve.wait_ge(ks_ps[f], c)
                        nc.vector.tensor_tensor(half(rhs[:, :], f), half(g.V[:, c, :], f),
                                                ps[:, 2 * f:2 * f + 2, 0:64].rearrange("p j (q e) -> p j q e", q=HG), ALU.subtract).then_inc(rhs_ok[f], 1)
                    else:
                        nc.vector.tensor_copy(half(rhs[:, :], f), half(g.V[:, 0, :], f)).then_inc(rhs_ok[f], 1)
                for f in range(2):
                    dve.wait_ge(vn_ps[f], c + 1)
                    if c >= NV:
                        dve.wait_ge(va_out[c % NV], 64 * (c // NV))
                    out = VA[:, c % NV, :, 0:HD].rearrange("p (q j) e -> p q j e", q=HG)[:, :, 2 * f:2 * f + 2, :]
                    nc.vector.tensor_copy(out, ps[:, 2 * f, P:2 * P].rearrange("p (q j e) -> p q j e", q=HG, j=2)).then_inc(vn_ok[f], 1)
                if c + 1 < NT:
                    for f in range(2):
                        dve.wait_ge(su_ps[f], c + 1)
                        r = slice(64 * f, 64 * f + 64)
                        nc.vector.tensor_tensor(S[r, :, :, :], S[r, :, :, :], ps[r, 4:8, 0:64].rearrange("p b (q e) -> p b q e", q=HG), ALU.add).then_inc(s_ok[f], 1)

        @block.sync
        def _(sp):
            for c in range(NT):
                for f in range(2):
                    sp.wait_ge(vn_ok[f], c + 1)
                for b in range(B):
                    i0 = R * (c % 4)
                    sp.dma_start(g.VN[i0:i0 + R, b, c // 4, :], VA[R * b:R * b + R, c % NV, :, :].rearrange("p h e -> p (h e)")).then_inc(va_out[c % NV], 16)
            for i in range(NV):
                sp.wait_ge(va_out[i], 64 * NT // NV)


MAX_UNITS = [(0, 4 * i, 4) for i in range(4)] + [(1, 2 * i, 2) for i in range(8)] + [(t, h, 1) for t in (2, 3) for h in range(H)]
NMU = len(MAX_UNITS)
STEPS = HG * 3 * 2
KEYS = [[(0, 0)], [(1, 0)], [(2, 0), (3, 256)]]
WIDTH = [512, 384, 384]


def max_units_at(step):
    last = STEPS - 2
    return range(NMU * step // last, NMU * (step + 1) // last) if step < last else range(0)


def phase_attention(nc, g, name, OT, shared_k, parts_k, k_row0, va):
    with ExitStack() as ctx:
        sb = lambda n, s, d=F32: ctx.enter_context(nc.sbuf_tensor(f"{name}_{n}", s, d))
        sem = semaphores(nc, ctx, f"{name}_")
        ps = g.ps
        NS = 3
        HK = 1 if shared_k else H
        QS = sb("q_stack", [P, NS, H, N], BF16)
        KS = sb("k_stack", [P, NS, HK, N], BF16)
        PT = sb("probs", [P, 4, 2, N])
        mx = sb("neg_max", [P, 4, H])
        mrem = sb("max_rem", [P, 4, H])
        mp = sb("max_parts", [P, 4, NPART, H], BF16)
        mT = sb("max_partsT", [NPART * H, N], BF16)
        stack = [sem(f"stack_loaded{i}") for i in range(NS)]
        mrow = [sem(f"max_rows_loaded{i}") for i in range(NS)]
        ones_ok, mu_ps, mu_ok, mp_ok, mt_ps, mt_sb = (sem("ones_rows"), sem("max_unit_psum"), sem("max_unit_reduced"), sem("max_parts"),
                                                      sem("maxT_psum"), sem("maxT_sbuf"))
        st_ps, exp_ok, pv_ok, ot_sb = sem("scoresT_psum"), sem("probs_ready"), sem("pv_done"), sem("out_group_sbuf")
        block = ctx.enter_context(nc.Block())

        def pv_at(S):
            return [(S - 3) // 2] if S >= 3 and S % 2 == 1 else []

        @block.sync
        def _(sp):
            for b in range(B):
                s = b % NS
                if b >= NS:
                    sp.wait_ge(st_ps, STEPS * (b - NS + 1))
                for r, (pq, pk) in enumerate(PAIRS):
                    src = bass.AP(tensor=g.parts_d.tensor, offset=pq * 4 * P * B * N + b * N, ap=[[B * N, HD], [HD * B * N, H], [1, N]])
                    sp.dma_start(QS[HD * r:HD * r + HD, s, :, :], src).then_inc(stack[s], 16)
                    src = bass.AP(tensor=parts_k.tensor, offset=(pk * 4 * P + k_row0) * B * N + b * N, ap=[[B * N, HD], [HD * B * N, HK], [1, N]])
                    sp.dma_start(KS[HD * r:HD * r + HD, s, :, :], src).then_inc(stack[s], 16)

        @block.gpsimd
        def _(pool):
            nc.gpsimd.memset(KS[KR:KRM, :, :, :], 1.0).then_inc(ones_ok, 1)
            for b in range(B):
                s = b % NS
                pool.wait_ge(mt_sb, b + 1)
                for p in range(NPART):
                    pool.dma_start(QS[KR + p:KR + p + 1, s, :, :], mT[H * p:H * p + H, :]).then_inc(mrow[s], 16)

        @block.tensor
        def _(pe):
            def max_unit(b, u):
                n = b * (NMU + 1) + u
                bank, s = n % 2, b % NS
                if u == 0:
                    pe.wait_ge(stack[s], 16 * 2 * len(PAIRS) * (b // NS + 1))
                if u >= 2:
                    pe.wait_ge(mu_ok, b * NMU + u - 1)
                elif b:
                    if u == 0:
                        pe.wait_ge(mu_ok, b * NMU)
                    else:
                        pe.wait_ge(mt_sb, b)
                if u == NMU:
                    pe.wait_ge(mp_ok, 4 * (b + 1))
                    out = ps[:, bank, :].bitcast(BF16)
                    for t in range(4):
                        last = nc.tensor.transpose(out[0:NPART * H, t * P:(t + 1) * P], mp[:, t, :, :].rearrange("p a h -> p (a h)"), g.idb[:, :])
                    last.then_inc(mt_ps, 1)
                    return
                t, h0, nh = MAX_UNITS[u]
                w = (t + 1) * P
                for h in range(h0, h0 + nh):
                    o = (h - h0) * w
                    kh = 0 if shared_k else h
                    nc.tensor.matmul(ps[:, bank, o:o + w], QS[0:KR, s, h, t * P:(t + 1) * P], KS[0:KR, s, kh, 0:w], start=True, stop=False)
                    last = nc.tensor.matmul(ps[:, bank, o + w - P:o + w], g.idb[:, :], g.maskq[:, :], start=False, stop=True)
                last.then_inc(mu_ps, 1)

            def score_unit(S):
                b, s = S // STEPS, S // STEPS % NS
                gq, ks, pr = S % STEPS // 6, S % 6 // 2, S % 2
                if S % STEPS == 0:
                    pe.wait_ge(mrow[s], 48 * (b // NS + 1))
                if S >= 2:
                    pe.wait_ge(exp_ok, S - 1)
                for e in range(2):
                    h = 4 * gq + 2 * pr + e
                    kh = 0 if shared_k else h
                    for kb, o in KEYS[ks]:
                        w = N - kb * P
                        bank = 2 + 2 * (S % 2) + e
                        nc.tensor.matmul(ps[:, bank, o:o + w], KS[0:KRM, s, kh, kb * P:(kb + 1) * P], QS[0:KRM, s, h, kb * P:N], start=True, stop=False)
                        last = nc.tensor.matmul(ps[:, bank, o:o + P], g.idb[:, :], g.maskk[:, :], start=False, stop=True)
                last.then_inc(st_ps, 1)

            def pv(n):
                og, ks = n // 3, n % 3
                b, gq = og // HG, og % HG
                pe.wait_ge(exp_ok, 2 * (n + 1))
                if ks == 0 and og >= 2:
                    pe.wait_ge(ot_sb, og - 1)
                for kb, o in KEYS[ks]:
                    w = N - kb * P
                    for j in range(4):
                        slot = (2 * n + j // 2) % 4
                        last = nc.tensor.matmul(ps[32 * j:32 * j + 32, 6 + og % 2, kb * P:N], va(b, kb, 4 * gq + j),
                                                PT[:, slot, j % 2, o:o + w], start=(kb == 0), stop=(kb == 3))
                last.then_inc(pv_ok, 1)

            pe.wait_ge(ones_ok, 1)
            for u in range(NMU + 1):
                max_unit(0, u)
            for S in range(B * STEPS):
                score_unit(S)
                for n in pv_at(S):
                    pv(n)
                if S // STEPS + 1 < B:
                    for u in max_units_at(S % STEPS):
                        max_unit(S // STEPS + 1, u)
                    if S % STEPS == STEPS - 1:
                        max_unit(S // STEPS + 1, NMU)
            pv(B * STEPS // 2 - 1)

        @block.vector
        def _(dve):
            def reduce_unit(b, u):
                t, h0, nh = MAX_UNITS[u]
                w = (t + 1) * P
                dve.wait_ge(mu_ps, b * NMU + u + 1)
                if b and u == 0:
                    dve.wait_ge(mp_ok, 4 * b)
                nc.vector.tensor_reduce(mx[:, t, h0:h0 + nh], ps[:, (b * (NMU + 1) + u) % 2, 0:nh * w].rearrange("p (h k) -> p h k", h=nh),
                                        AX.X, ALU.max, negate=True).then_inc(mu_ok, 1)

            def split_max(b):
                dve.wait_ge(mu_ok, NMU * (b + 1))
                if b:
                    dve.wait_ge(mt_ps, b)
                nc.vector.tensor_copy(mp[:, :, 0, :], mx[:, :, :]).then_inc(mp_ok, 1)
                dve.wait_ge(mp_ok, 4 * b + 1)
                nc.vector.tensor_tensor(mrem[:, :, :], mx[:, :, :], mp[:, :, 0, :], ALU.subtract).then_inc(mp_ok, 1)
                dve.wait_ge(mp_ok, 4 * b + 2)
                nc.vector.tensor_copy(mp[:, :, 1, :], mrem[:, :, :]).then_inc(mp_ok, 1)
                dve.wait_ge(mp_ok, 4 * b + 3)
                nc.vector.tensor_tensor(mp[:, :, 2, :], mrem[:, :, :], mp[:, :, 1, :], ALU.subtract).then_inc(mp_ok, 1)

            def out_group(n):
                og = n // 3
                b, gq = og // HG, og % HG
                dve.wait_ge(pv_ok, n + 1)
                nc.vector.tensor_copy(OT[:, gq, :, R * b:R * b + R], ps[:, 6 + og % 2, :].rearrange("p (c i) -> p c i", c=NT)).then_inc(ot_sb, 1)

            for u in range(NMU):
                reduce_unit(0, u)
            split_max(0)
            for S in range(B * STEPS):
                if S // STEPS + 1 < B:
                    for u in max_units_at(S % STEPS):
                        reduce_unit(S // STEPS + 1, u)
                    if S % STEPS == STEPS - 2:
                        split_max(S // STEPS + 1)
                for n in pv_at(S):
                    if n % 3 == 2:
                        out_group(n)
            out_group(B * STEPS // 2 - 1)

        @block.scalar
        def _(act):
            def maxT(b):
                act.wait_ge(mt_ps, b + 1)
                if b:
                    act.wait_ge(mrow[(b - 1) % NS], 48 * ((b - 1) // NS + 1))
                nc.scalar.copy(mT[:, :], ps[:, (b * (NMU + 1) + NMU) % 2, :].bitcast(BF16)[0:NPART * H, 0:N]).then_inc(mt_sb, 1)

            maxT(0)
            for S in range(B * STEPS):
                n = S // 2
                act.wait_ge(st_ps, S + 1)
                if S >= 4:
                    act.wait_ge(pv_ok, n - 1)
                w = WIDTH[S % 6 // 2]
                bank = 2 + 2 * (S % 2)
                nc.scalar.activation(PT[:, S % 4, :, 0:w], ps[:, bank:bank + 2, 0:w], ACT.Exp, scale=SCALE).then_inc(exp_ok, 1)
                if S // STEPS + 1 < B and S % STEPS == STEPS - 1:
                    maxT(S // STEPS + 1)


class LayerNorm:

    def __init__(self, nc, ctx, name, eps):
        self.nc = nc
        sb = lambda n, s: ctx.enter_context(nc.sbuf_tensor(f"{name}_{n}", s, F32))
        sem = semaphores(nc, ctx, f"{name}_")
        self.eps = eps
        self.st, self.mv, self.sd, self.rs = sb("stats", [P, 4, 6]), sb("mean_var", [P, 4, 2]), sb("std", [P, 4, 1]), sb("rstd", [P, 4, 1])
        self.nm, self.nm_ok = sb("neg_mean_rstd", [P, 4, 1]), sem("neg_mean_rstd_ok")
        self.st_ok, self.mv_ok, self.sd_ok, self.rs_ok, self.y_ok = sem("stats_ok"), sem("mean_var_ok"), sem("std_ok"), sem("rstd_ok"), sem("normalized")

    def stats(self, dve, n, x):
        nc, s = self.nc, n % 4
        if n >= 4:
            dve.wait_ge(self.y_ok, n - 3)
        nc.vector.bn_stats(self.st[:, s, :], x).then_inc(self.st_ok, 1)

    def mean_var(self, dve, n):
        dve.wait_ge(self.st_ok, n + 1)
        self.nc.vector.bn_aggr(self.mv[:, n % 4, :], self.st[:, n % 4, :]).then_inc(self.mv_ok, 1)

    def std(self, act, n):
        act.wait_ge(self.mv_ok, n + 1)
        if n >= 4:
            act.wait_ge(self.rs_ok, n - 3)
        self.nc.scalar.activation(self.sd[:, n % 4, :], self.mv[:, n % 4, 1:2], ACT.Sqrt, bias=self.eps).then_inc(self.sd_ok, 1)

    def rstd(self, dve, n):
        dve.wait_ge(self.sd_ok, n + 1)
        self.nc.vector.reciprocal(self.rs[:, n % 4, :], self.sd[:, n % 4, :]).then_inc(self.rs_ok, 1)

    def shift(self, dve, n):
        s = n % 4
        dve.wait_ge(self.rs_ok, n + 1)
        self.nc.vector.scalar_tensor_tensor(out=self.nm[:, s, :], in0=self.mv[:, s, 0:1], scalar=-1.0, in1=self.rs[:, s, :],
                                            op0=ALU.mult, op1=ALU.mult).then_inc(self.nm_ok, 1)

    def apply_act(self, act, n, out, x):
        s = n % 4
        act.wait_ge(self.nm_ok, n + 1)
        self.nc.scalar.activation(out, x, ACT.Identity, scale=self.rs[:, s, :], bias=self.nm[:, s, :]).then_inc(self.y_ok, 1)

    def apply(self, dve, n, out, x):
        s = n % 4
        dve.wait_ge(self.rs_ok, n + 1)
        self.nc.vector.tensor_scalar(out, x, self.mv[:, s, 0:1], self.rs[:, s, :], ALU.subtract, ALU.mult).then_inc(self.y_ok, 1)


def phase_out_proj(nc, g, name, OT, load_w, bias):
    with ExitStack() as ctx:
        sb = lambda n, s, d=F32: ctx.enter_context(nc.sbuf_tensor(f"{name}_{n}", s, d))
        sem = semaphores(nc, ctx, f"{name}_")
        ps = g.ps
        rec = sb("inv_sum", [P, 2, H])
        on = sb("heads", [P, 2, D])
        onT = sb("headsT", [P, 2, KD, P])
        o_ps, rec_ok, on_ok, t_ps, t_sb, y_ps, u_ok, b_ok = (sem("rows_psum"), sem("inv_sum_ok"), sem("heads_ok"), sem("headsT_psum"), sem("headsT_sbuf"),
                                                           sem("proj_psum"), sem("residual_added"), sem("bias_added"))
        w_ld = sem("w_loaded")
        ln = LayerNorm(nc, ctx, name, g.eps[:, 0:1])
        W = load_w(None, None)
        block = ctx.enter_context(nc.Block())

        @block.sync
        def _(sp):
            load_w(sp, w_ld)

        @block.tensor
        def _(pe):
            def rows(c):
                if c >= 2:
                    pe.wait_ge(on_ok, c - 1)
                for q in range(HG):
                    last = nc.tensor.transpose(ps[:, c % 2, q * P:(q + 1) * P], OT[:, q, c, :], g.idf[:, :])
                last.then_inc(o_ps, 1)

            def headsT(c):
                pe.wait_ge(on_ok, c + 1)
                if c >= 2:
                    pe.wait_ge(t_sb, c - 1)
                for k in range(KD):
                    last = nc.tensor.transpose(ps[:, 2 + c % 2, k * P:(k + 1) * P], on[:, c % 2, k * P:(k + 1) * P], g.idf[:, :])
                last.then_inc(t_ps, 1)

            def project(c):
                if c == 0:
                    pe.wait_ge(w_ld, 16)
                pe.wait_ge(t_sb, c + 1)
                if c >= 2:
                    pe.wait_ge(u_ok, c - 1)
                for k in range(KD):
                    last = nc.tensor.matmul(ps[:, 4 + c % 2, 0:D], onT[:, c % 2, k, :], W[:, k, :], start=(k == 0), stop=(k == KD - 1))
                last.then_inc(y_ps, 1)

            rows(0)
            for c in range(NT):
                if c + 1 < NT:
                    rows(c + 1)
                headsT(c)
                if c:
                    project(c - 1)
            project(NT - 1)

        @block.vector
        def _(dve):
            def heads(c):
                dve.wait_ge(o_ps, c + 1)
                if c >= 2:
                    dve.wait_ge(t_ps, c - 1)
                v = ps[:, c % 2, :].rearrange("p (h e) -> p h e", h=H)
                nc.vector.reciprocal(rec[:, c % 2, :], v[:, :, HD]).then_inc(rec_ok, 1)
                dve.wait_ge(rec_ok, c + 1)
                nc.vector.tensor_tensor(on[:, c % 2, :].rearrange("p (h e) -> p h e", h=H), v[:, :, 0:HD],
                                        bcast(rec[:, c % 2, :], [[1, H], [0, HD]]), ALU.mult).then_inc(on_ok, 1)

            def residual(c):
                dve.wait_ge(y_ps, c + 1)
                if bias is not None:
                    dve.wait_ge(b_ok, c + 1)
                nc.vector.tensor_tensor(g.X[:, c, :], g.X[:, c, :], ps[:, 4 + c % 2, 0:D], ALU.add).then_inc(u_ok, 1)

            for c in range(NT + 4):
                if 4 <= c:
                    ln.rstd(dve, c - 4)
                if 2 <= c < NT + 2:
                    residual(c - 2)
                if c < NT:
                    heads(c)
                if 2 <= c < NT + 2:
                    dve.wait_ge(u_ok, c - 1)
                    ln.stats(dve, c - 2, g.X[:, c - 2, :])
                if 4 <= c:
                    ln.apply(dve, c - 4, g.X[:, c - 4, :], g.X[:, c - 4, :])
                if 2 <= c < NT + 2:
                    ln.mean_var(dve, c - 2)

        @block.scalar
        def _(act):
            for c in range(NT):
                act.wait_ge(t_ps, c + 1)
                if c >= 2:
                    act.wait_ge(y_ps, c - 1)
                nc.scalar.copy(onT[:, c % 2, :, :], ps[:, 2 + c % 2, 0:KD * P].rearrange("p (k m) -> p k m", k=KD)).then_inc(t_sb, 1)
                if c >= 3:
                    ln.std(act, c - 3)
            for c in range(NT - 3, NT):
                ln.std(act, c)

        @block.gpsimd
        def _(pool):
            if bias is not None:
                for c in range(NT):
                    nc.gpsimd.tensor_tensor(g.X[:, c, :], g.X[:, c, :], bias[:, :], ALU.add).then_inc(b_ok, 1)


def alloc_ffn_weights(nc, g, ctx):
    F4 = 4 * D
    sb = lambda n, s: ctx.enter_context(nc.sbuf_tensor(f"wt_{n}", s, F32))
    g.ew, g.epw, g.eb = sb("ent_w", [P, 2, KD, F4]), sb("ent_pw", [P, 2, F4 // P, D]), sb("ent_b", [2 * F4 // P, P])
    g.pw, g.ph, g.pb = sb("path_w", [P, 2, 2, KD, D]), sb("phase", [P, 2, 4 * D]), sb("path_b", [P, 4 * D])


def load_ffn_weights(sp, g):
    d = g.d
    sp.dma_start(g.ph[:, 0, :], rows_bcast(d["L0_ffn_phase"], 0, 4 * D)).then_inc(g.phase_ld, 16)
    for l in range(2):
        sp.dma_start(g.ew[:, l, :, :], d["L0_ffn_ent_w"][l].rearrange("(k p) n -> p k n", p=P)).then_inc(g.ffn_ld, 16)
        sp.dma_start(g.epw[:, l, :, :], d["L0_ffn_ent_pw"][l].rearrange("(k p) n -> p k n", p=P)).then_inc(g.ffn_ld, 16)
        for q in range(2):
            sp.dma_start(g.pw[:, l, q, :, :], d["L0_ffn_path_w"][l, q].rearrange("(k p) n -> p k n", p=P)).then_inc(g.ffn_ld, 16)
    sp.dma_start(g.eb[:, :], d["L0_ffn_ent_b"].rearrange("l (k p) -> (l k) p", p=P)).then_inc(g.ffn_ld, 16)
    sp.dma_start(g.pb[:, :], rows_bcast(d["L0_ffn_path_b"], 0, 4 * D)).then_inc(g.ffn_ld, 16)
    sp.dma_start(g.Wap[:, :, 0:D], d["L0_ffn_amp_w"].rearrange("(k p) n -> p k n", p=P)).then_inc(g.ffn_ld, 16)
    sp.dma_start(g.Wap[:, :, D:], d["L0_ffn_ph_w"].rearrange("(k p) n -> p k n", p=P)).then_inc(g.ffn_ld, 16)
    sp.dma_start(g.bap[:, 0:D], rows_bcast(d["L0_ffn_amp_b"], 0, D)).then_inc(g.ffn_ld, 16)
    sp.dma_start(g.bap[:, D:], rows_bcast(d["L0_ffn_ph_b"], 0, D)).then_inc(g.ffn_ld, 16)
    for l in range(2):
        sp.dma_start(g.bst[:, 2 * l, :], rows_bcast(d["L0_ffn_ent_pb"], l * D, D)).then_inc(g.ffn_ld, 16)
        for s, (gm, bt) in enumerate((("ln3_g", "ln3_b"), ("ln4_g", "ln4_b"))):
            sp.dma_start(g.gam[:, 2 * l + s, :], rows_bcast(d["L0_ffn_" + gm], l * D, D)).then_inc(g.ffn_ld, 16)
            sp.dma_start(g.bet[:, 2 * l + s, :], rows_bcast(d["L0_ffn_" + bt], l * D, D)).then_inc(g.ffn_ld, 16)


def phase_weights(nc, g):
    F4 = 4 * D
    KF = F4 // P
    with ExitStack() as ctx:
        sb = lambda n, s, d=F32: ctx.enter_context(nc.sbuf_tensor(f"wt_{n}", s, d))
        sem = semaphores(nc, ctx, f"wt_")
        ps = g.ps
        ew, epw, eb, pw, ph, pb = g.ew, g.epw, g.eb, g.pw, g.ph, g.pb
        ewT, ebT, kk = sb("ent_wT", [P, 2, KF, D]), sb("ent_bT", [P, 2 * KF]), sb("turns", [P, 4 * D])
        ld, ldp = g.ffn_ld, g.phase_ld
        mod_st, sin_ok, tp, te, wp, we = (sem("modulation"), sem("sines"), sem("transposed"), sem("evacuated"), sem("product"), sem("product_out"))
        block = ctx.enter_context(nc.Block())

        @block.sync
        def _(sp):
            load_l1_qkv(sp, g)

        NLD = 8 + 6 + 10

        @block.vector
        def _(dve):
            p0, p1 = ph[:, 0, :], ph[:, 1, :]
            n = [0]

            def step(ins):
                n[0] += 1
                ins.then_inc(mod_st, 1)
                dve.wait_ge(mod_st, n[0])

            dve.wait_ge(ldp, 16)
            MAGIC = 12582912.0
            step(nc.vector.tensor_scalar(kk[:, :], p0, 1.0 / (2 * PI), None, ALU.mult))
            step(nc.vector.tensor_scalar(kk[:, :], kk[:, :], MAGIC, None, ALU.add))
            step(nc.vector.tensor_scalar(kk[:, :], kk[:, :], -MAGIC, None, ALU.add))
            c1 = 6.28125
            c2 = float((np.array([2 * PI - c1], np.float32).view(np.uint32) & np.uint32(0xFFFFF000)).view(np.float32)[0])
            c3 = 2 * PI - c1 - c2
            for cc in (c1, c2, c3):
                step(nc.vector.scalar_tensor_tensor(out=p0, in0=kk[:, :], scalar=-cc, in1=p0, op0=ALU.mult, op1=ALU.add))
            step(nc.vector.tensor_scalar(p0, p0, 3.1415925, -3.1415925, ALU.min, ALU.max))
            step(nc.vector.scalar_tensor_tensor(out=p1, in0=p0, scalar=-1.0, in1=p0, op0=ALU.mult, op1=ALU.min))
            step(nc.vector.tensor_scalar(p1, p1, PI / 2, None, ALU.add))
            dve.wait_ge(sin_ok, 1)
            step(nc.vector.tensor_tensor(p0, p0, p1, ALU.add))
            dve.wait_ge(ld, 16 * NLD)
            for l in range(2):
                mod = [p0[:, (2 * l + q) * D:(2 * l + q + 1) * D] for q in range(2)]
                for q in range(2):
                    step(nc.vector.tensor_tensor(pw[:, l, q, :, :], pw[:, l, q, :, :], bcast(mod[q], [[0, KD], [1, D]]), ALU.mult))
                step(nc.vector.tensor_tensor(g.Wst[:, 2 * l + 1, :, :], pw[:, l, 0, :, :], pw[:, l, 1, :, :], ALU.add))
            step(nc.vector.tensor_tensor(pb[:, :], pb[:, :], p0, ALU.mult))
            for l in range(2):
                step(nc.vector.tensor_tensor(g.bst[:, 2 * l + 1, :], pb[:, 2 * l * D:(2 * l + 1) * D], pb[:, (2 * l + 1) * D:(2 * l + 2) * D], ALU.add))
            for l in range(2):
                dve.wait_ge(wp, 3 * l + 3)
                for k in range(KD):
                    nc.vector.tensor_copy(g.Wst[:, 2 * l, k, :], ps[:, 4 + k, 0:D]).then_inc(we, 1)
                nc.vector.tensor_tensor(g.bst[:, 2 * l, :], g.bst[:, 2 * l, :], ps[:, 6, 0:D], ALU.add).then_inc(we, 1)

        @block.scalar
        def _(act):
            act.wait_ge(mod_st, 9)
            nc.scalar.activation(ph[:, :, :], ph[:, :, :], ACT.Sin).then_inc(sin_ok, 1)
            for i in range(2 * KF + 1):
                act.wait_ge(tp, i + 1)
                if i < 2 * KF:
                    l, k = i // KF, i % KF
                    nc.scalar.copy(ewT[:, l, k, :], ps[:, i % 4, 0:D]).then_inc(te, 1)
                else:
                    nc.scalar.copy(ebT[:, :], ps[:, i % 4, 0:2 * KF]).then_inc(te, 1)

        @block.tensor
        def _(pe):
            pe.wait_ge(ld, 16 * NLD)
            for i in range(2 * KF + 1):
                if i >= 4:
                    pe.wait_ge(te, i - 3)
                if i < 2 * KF:
                    l, k = i // KF, i % KF
                    for m in range(KD):
                        last = nc.tensor.transpose(ps[:, i % 4, m * P:(m + 1) * P], ew[:, l, m, k * P:(k + 1) * P], g.idf[:, :])
                else:
                    last = nc.tensor.transpose(ps[:, i % 4, 0:2 * KF], eb[:, :], g.idf[0:2 * KF, 0:2 * KF])
                last.then_inc(tp, 1)
            pe.wait_ge(te, 2 * KF + 1)
            for l in range(2):
                if l:
                    pe.wait_ge(we, 3)
                for m in range(KD):
                    for k in range(KF):
                        last = nc.tensor.matmul(ps[:, 4 + m, 0:D], ewT[:, l, k, m * P:(m + 1) * P], epw[:, l, k, :], start=(k == 0), stop=(k == KF - 1))
                    last.then_inc(wp, 1)
                for k in range(KF):
                    last = nc.tensor.matmul(ps[:, 6, 0:D], bcast(ebT[:, l * KF + k:l * KF + k + 1], [[0, P]]), epw[:, l, k, :], start=(k == 0), stop=(k == KF - 1))
                last.then_inc(wp, 1)


def phase_ffn(nc, g):
    with ExitStack() as ctx:
        sb = lambda n, s, d=F32: ctx.enter_context(nc.sbuf_tensor(f"ffn_{n}", s, d))
        sem = semaphores(nc, ctx, f"ffn_")
        ps = g.ps
        ST = 4
        xT = sb("xT", [P, 4, KD, P])
        Z = sb("amp_phase", [P, NT, 2 * D])
        Hh = sb("h_rows", [P, NT, D])
        tb = sb("cos_arg", [P, 2, G4, D])
        NB = 6
        hb = sb("residual", [P, NB, D])
        pih = sb("half_pi", [P, 1])
        t_ps, t_sb, z_ps, z_ok, sg_ok, ar_ok, sn_ok, h0_ok, c_ok = (sem("xT_psum"), sem("xT_sbuf"), sem("z_psum"), sem("z_rows"), sem("sigmoid_tanh"),
                                                                  sem("sine_args"), sem("sines"), sem("h_sum"), sem("const"))
        hb_ok, y_ps, u_ok, sc_ok, h_ok, fx_ok = (sem("h_plus_bias"), sem("y_psum"), sem("u_ok"), sem("scaled"), sem("h_ok"), sem("x_plus_h"))
        ln = LayerNorm(nc, ctx, "ffnln", g.eps[:, 0:1])
        block = ctx.enter_context(nc.Block())
        NH = ST * NT

        @block.tensor
        def _(pe):
            def xpose(n):
                if n >= 2:
                    pe.wait_ge(t_sb, n - 1)
                if n < NT:
                    src = g.X[:, n, :]
                elif n < 2 * NT:
                    pe.wait_ge(h0_ok, 2 * ((n - NT) // G4 + 1))
                    src = Hh[:, n - NT, :]
                else:
                    pe.wait_ge(h_ok, n - 2 * NT + 1)
                    src = Hh[:, n % NT, :]
                for k in range(KD):
                    last = nc.tensor.transpose(ps[:, n % 2, k * P:(k + 1) * P], src[:, k * P:(k + 1) * P], g.idf[:, :])
                last.then_inc(t_ps, 1)

            def dense(n):
                pe.wait_ge(t_sb, n + 1)
                if n < NT:
                    if n >= 2:
                        pe.wait_ge(z_ok, n - 1)
                    for k in range(KD):
                        last = nc.tensor.matmul(ps[:, 2 + n % 2, :], xT[:, n % 4, k, :], g.Wap[:, k, :], start=(k == 0), stop=(k == KD - 1))
                    last.then_inc(z_ps, 1)
                else:
                    m = n - NT
                    if m >= 4:
                        pe.wait_ge(u_ok, m - 3)
                    for k in range(KD):
                        last = nc.tensor.matmul(ps[:, 4 + m % 4, 0:D], xT[:, n % 4, k, :], g.Wst[:, m // NT, k, :], start=(k == 0), stop=(k == KD - 1))
                    last.then_inc(y_ps, 1)

            xpose(0)
            for n in range(NT + NH):
                if n + 1 < NT + NH and n != NT - 1:
                    xpose(n + 1)
                dense(n)
                if n == NT - 1:
                    xpose(NT)

        @block.scalar
        def _(act):
            def evac(n):
                act.wait_ge(t_ps, n + 1)
                if 4 <= n < NT + 4:
                    act.wait_ge(z_ps, n - 3)
                elif n >= NT + 4:
                    act.wait_ge(y_ps, n - NT - 3)
                nc.scalar.copy(xT[:, n % 4, :, :], ps[:, n % 2, 0:KD * P].rearrange("p (k m) -> p k m", k=KD)).then_inc(t_sb, 1)

            def normalize(m):
                x = hb[:, m % NB, :] if m < NH else g.X[:, m - NH, :]
                ln.apply_act(act, m, x, x)

            for n in range(NT):
                evac(n)
            for q in range(NG):
                gs = slice(q * G4, (q + 1) * G4)
                act.wait_ge(z_ok, (q + 1) * G4)
                nc.scalar.activation(Z[:, gs, 0:D], Z[:, gs, 0:D], ACT.Sigmoid).then_inc(sg_ok, 1)
                nc.scalar.activation(Z[:, gs, D:], Z[:, gs, D:], ACT.Tanh).then_inc(sg_ok, 1)
            act.wait_ge(c_ok, 1)
            for q in range(NG):
                gs = slice(q * G4, (q + 1) * G4)
                act.wait_ge(ar_ok, 2 * (q + 1))
                nc.scalar.activation(Z[:, gs, D:], Z[:, gs, D:], ACT.Sin).then_inc(sn_ok, 1)
                nc.scalar.activation(tb[:, q % 2, :, :], tb[:, q % 2, :, :], ACT.Sin, bias=pih[:, 0:1]).then_inc(sn_ok, 1)
            for n in range(NT, NT + NH):
                evac(n)
                if n >= NT + 3:
                    ln.std(act, n - NT - 3)
                if n >= NT + 4:
                    normalize(n - NT - 4)
            for m in range(NH - 3, NH + NT):
                ln.std(act, m)
                normalize(m - 1)
            normalize(NH + NT - 1)

        @block.vector
        def _(dve):
            nc.vector.memset(pih[:, :], PI / 2).then_inc(c_ok, 1)
            for n in range(NT):
                dve.wait_ge(z_ps, n + 1)
                nc.vector.tensor_tensor(Z[:, n, :], ps[:, 2 + n % 2, :], g.bap[:, :], ALU.add).then_inc(z_ok, 1)
            for q in range(NG):
                gs = slice(q * G4, (q + 1) * G4)
                dve.wait_ge(sg_ok, 2 * (q + 1))
                nc.vector.tensor_scalar(Z[:, gs, D:], Z[:, gs, D:], 3.1415925, None, ALU.mult).then_inc(ar_ok, 1)
                dve.wait_ge(ar_ok, 2 * q + 1)
                if q >= 2:
                    dve.wait_ge(h0_ok, 2 * (q - 1))
                nc.vector.scalar_tensor_tensor(out=tb[:, q % 2, :, :], in0=Z[:, gs, D:], scalar=-1.0, in1=Z[:, gs, D:], op0=ALU.mult, op1=ALU.min).then_inc(ar_ok, 1)

            def residual(m):
                if m < NH:
                    dve.wait_ge(y_ps, m + 1)
                    dve.wait_ge(hb_ok, m + 1)
                    nc.vector.tensor_tensor(hb[:, m % NB, :], hb[:, m % NB, :], ps[:, 4 + m % 4, 0:D], ALU.add).then_inc(u_ok, 1)

            def stats(m):
                if m < NH:
                    dve.wait_ge(u_ok, m + 1)
                    ln.stats(dve, m, hb[:, m % NB, :])
                else:
                    dve.wait_ge(fx_ok, m - NH + 1)
                    ln.stats(dve, m, g.X[:, m - NH, :])

            def scale(m):
                if m < NH:
                    dve.wait_ge(ln.y_ok, m + 1)
                    dve.wait_ge(t_ps, NT + m + 1)
                    nc.vector.tensor_tensor(Hh[:, m % NT, :], hb[:, m % NB, :], g.gam[:, m // NT, :], ALU.mult).then_inc(sc_ok, 1)

            for m in range(NH + NT + 2):
                if m < NH + NT:
                    residual(m)
                if m >= 2:
                    ln.rstd(dve, m - 2)
                if m < NH + NT:
                    stats(m)
                if m >= 2:
                    ln.shift(dve, m - 2)
                if m >= 3:
                    scale(m - 3)
                if m < NH + NT:
                    ln.mean_var(dve, m)

        @block.gpsimd
        def _(pool):
            for q in range(NG):
                gs = slice(q * G4, (q + 1) * G4)
                pool.wait_ge(sn_ok, 2 * (q + 1))
                nc.gpsimd.tensor_tensor(tb[:, q % 2, :, :], tb[:, q % 2, :, :], Z[:, gs, D:], ALU.add).then_inc(h0_ok, 1)
                pool.wait_ge(h0_ok, 2 * q + 1)
                nc.gpsimd.tensor_tensor(Hh[:, gs, :], tb[:, q % 2, :, :], Z[:, gs, 0:D], ALU.mult).then_inc(h0_ok, 1)

            def add_bias(m):
                if m >= NB:
                    pool.wait_ge(sc_ok, m - NB + 1)
                if m < NT:
                    pool.wait_ge(h0_ok, 2 * (m // G4 + 1))
                else:
                    pool.wait_ge(h_ok, m - NT + 1)
                nc.gpsimd.tensor_tensor(hb[:, m % NB, :], Hh[:, m % NT, :], g.bst[:, m // NT, :], ALU.add).then_inc(hb_ok, 1)

            def add_beta(m):
                pool.wait_ge(sc_ok, m + 1)
                nc.gpsimd.tensor_tensor(Hh[:, m % NT, :], Hh[:, m % NT, :], g.bet[:, m // NT, :], ALU.add).then_inc(h_ok, 1)

            def final_sum(c):
                pool.wait_ge(h_ok, NH - NT + c + 1)
                nc.gpsimd.tensor_tensor(g.X[:, c, :], g.X[:, c, :], Hh[:, c, :], ALU.add).then_inc(fx_ok, 1)

            for m in range(NB - 1):
                add_bias(m)
            for m in range(NH):
                add_beta(m)
                if m + NB - 1 < NH:
                    add_bias(m + NB - 1)
                if m >= NH - NT:
                    final_sum(m - (NH - NT))


def load_l1_qkv(sp, g):
    d, NO = g.d, D + 2 * HD
    w = d["L1_attn_c_attn_w"]
    for j in range(2):
        sp.dma_start(g.ca[:, j, :], w[j * P:(j + 1) * P, :]).then_inc(g.l1_ld, 16)
    sp.dma_start(g.ca[0:2 * HD, 2, :], w[D:NO, :]).then_inc(g.l1_ld, 16)
    sp.dma_start(g.cp[:, :, :], d["L1_attn_c_proj_w"].rearrange("(k p) n -> p k n", p=P)).then_inc(g.l1_ld, 16)
    cb = d["L1_attn_c_attn_b"]
    for j in range(2):
        sp.dma_start(g.q_bias[:, j:j + 1], bass.AP(tensor=cb.tensor, offset=j * P, ap=[[1, P], [1, 1]])).then_inc(g.l1_ld, 16)
    sp.dma_start(g.k_bias[:, :], bass.AP(tensor=cb.tensor, offset=D, ap=[[1, HD], [1, 1]])).then_inc(g.l1_ld, 16)
    sp.dma_start(g.v_bias[:, :], rows_bcast(cb, D + HD, HD)).then_inc(g.l1_ld, 16)
    sp.dma_start(g.cpb[:, :], rows_bcast(d["L1_attn_c_proj_b"], 0, D)).then_inc(g.l1_ld, 16)


def phase_l1_qkv(nc, g):
    with ExitStack() as ctx:
        sb = lambda n, s, d=F32: ctx.enter_context(nc.sbuf_tensor(f"l1q_{n}", s, d))
        sem = semaphores(nc, ctx, f"l1q_")
        ps = g.ps
        NO = D + 2 * HD
        ca, cp, qb, kb_, vb = g.ca, g.cp, g.q_bias, g.k_bias, g.v_bias
        caT = sb("c_attnT", [P, KD, NO])
        xT = sb("xT", [P, KD, B, N])
        part = [sb(f"part{p}", [P, 3, B * N], BF16) for p in range(NPART)]
        rem = sb("rem", [P, 2, N])
        ld = g.l1_ld
        w_ps, w_sb, t_ps, t_sb, q_ps, p1_ok, r_ok, p2_ok, p3_ok, st, v_ps, v_ok, one = (
            sem("wT_psum"), sem("wT_sbuf"), sem("xT_psum"), sem("xT_sbuf"), sem("qT_psum"), sem("part1"), sem("rem1"),
            sem("part2"), sem("part3"), sem("stored"), sem("v_psum"), sem("v_ok"), sem("ones"))
        block = ctx.enter_context(nc.Block())
        d = g.d
        OUT = [(0, P, 0), (1, P, P), (2, HD, D)]
        NU = len(OUT) * B

        @block.sync
        def _(sp):
            sp.wait_ge(p3_ok, NU)
            for p in range(NPART):
                sp.dma_start(g.parts_d[p, 0:2].rearrange("x p n -> p x n"), part[p][:, 0:2, :]).then_inc(st, 16)
                sp.dma_start(g.parts_d[p, 2, 0:HD, :], part[p][0:HD, 2, :]).then_inc(st, 16)
            sp.wait_ge(st, 32 * NPART)

        @block.tensor
        def _(pe):
            pe.wait_ge(ld, 16 * 9)
            for j in range(5):
                if j >= 2:
                    pe.wait_ge(w_sb, j - 1)
                n = P if j != 2 else 2 * HD
                for k in range(KD):
                    src = ca[0:n, j, k * P:(k + 1) * P] if j < 3 else cp[:, j - 3, k * P:(k + 1) * P]
                    last = nc.tensor.transpose(ps[:, j % 2, k * P:k * P + n], src, g.idf[0:n, 0:n])
                last.then_inc(w_ps, 1)
            for c in range(NT):
                if c >= 2:
                    pe.wait_ge(t_sb, c - 1)
                for k in range(KD):
                    last = nc.tensor.transpose(ps[:, 2 + c % 2, k * P:(k + 1) * P], g.X[:, c, k * P:(k + 1) * P], g.idf[:, :])
                last.then_inc(t_ps, 1)
            pe.wait_ge(t_sb, NT)
            pe.wait_ge(w_sb, 5)
            for b in range(B):
                for t in range(4):
                    i = 4 * b + t
                    for k in range(KD):
                        last = nc.tensor.matmul(ps[:, 6, i * HD:(i + 1) * HD], xT[:, k, b, t * P:(t + 1) * P], caT[:, k, D + HD:NO], start=(k == 0), stop=(k == KD - 1))
            last.then_inc(v_ps, 1)
            for u in range(NU):
                x, n, c0 = OUT[u // B]
                b = u % B
                if u >= 2:
                    pe.wait_ge(r_ok, u - 1)
                for k in range(KD):
                    last = nc.tensor.matmul(ps[0:n, 4 + u % 2, :], caT[:, k, c0:c0 + n], xT[:, k, b, :], start=(k == 0), stop=(k == KD - 1))
                last.then_inc(q_ps, 1)

        @block.scalar
        def _(act):
            for j in range(5):
                act.wait_ge(w_ps, j + 1)
                n = P if j != 2 else 2 * HD
                dst = caT[:, :, j * P:j * P + n] if j < 3 else g.cpT[:, :, (j - 3) * P:(j - 2) * P]
                nc.scalar.copy(dst, ps[:, j % 2, 0:KD * P].rearrange("p (k m) -> p k m", k=KD)[:, :, 0:n]).then_inc(w_sb, 1)
            for c in range(NT):
                act.wait_ge(t_ps, c + 1)
                nc.scalar.copy(xT[:, :, :, c * R:(c + 1) * R], ps[:, 2 + c % 2, 0:KD * P].rearrange("p (k b i) -> p k b i", k=KD, b=B)).then_inc(t_sb, 1)
            for u in range(NU):
                x, n, c0 = OUT[u // B]
                b = u % B
                act.wait_ge(q_ps, u + 1)
                bias = qb[:, x:x + 1] if x < 2 else kb_[:, 0:1]
                nc.scalar.activation(part[0][0:n, x, b * N:(b + 1) * N], ps[0:n, 4 + u % 2, :], ACT.Identity, bias=bias).then_inc(p1_ok, 1)

        @block.vector
        def _(dve):
            nc.vector.memset(g.VA1[:, :, :], 1.0).then_inc(one, 1)
            dve.wait_ge(one, 1)
            dve.wait_ge(v_ps, 1)
            nc.vector.tensor_tensor(g.VA1[:, :, 0:HD], ps[:, 6, 0:16 * HD].rearrange("p (t e) -> p t e", e=HD), bcast(vb[:, :], [[0, 16], [1, HD]]), ALU.add).then_inc(v_ok, 1)
            for u in range(NU):
                x, n, c0 = OUT[u // B]
                b = u % B
                dve.wait_ge(p1_ok, u + 1)
                if u >= 2:
                    dve.wait_ge(p3_ok, u - 1)
                bias = qb[:, x:x + 1] if x < 2 else kb_[:, 0:1]
                nc.vector.scalar_tensor_tensor(out=rem[0:n, u % 2, :], in0=ps[0:n, 4 + u % 2, :], scalar=bias, in1=part[0][0:n, x, b * N:(b + 1) * N],
                                               op0=ALU.add, op1=ALU.subtract).then_inc(r_ok, 1)

        @block.gpsimd
        def _(pool):
            for u in range(NU):
                x, n, c0 = OUT[u // B]
                bs = slice((u % B) * N, (u % B + 1) * N)
                pool.wait_ge(r_ok, u + 1)
                nc.gpsimd.tensor_copy(part[1][0:n, x, bs], rem[0:n, u % 2, :]).then_inc(p2_ok, 1)
                pool.wait_ge(p2_ok, u + 1)
                nc.gpsimd.tensor_tensor(part[2][0:n, x, bs], rem[0:n, u % 2, :], part[1][0:n, x, bs], ALU.subtract).then_inc(p3_ok, 1)


def phase_moe(nc, g):
    with ExitStack() as ctx:
        sb = lambda n, s, d=F32: ctx.enter_context(nc.sbuf_tensor(f"moe_{n}", s, d))
        sem = semaphores(nc, ctx, f"moe_")
        ps = g.ps
        We, Wg, be = g.We, g.Wg, g.be
        xT = sb("xT", [P, NT, KD, P])
        lg, pr, rk, cb = sb("logits", [P, NT, E]), sb("exps", [P, NT, E]), sb("rank", [P, NT, E]), sb("combine", [P, NT, E])
        mxl, sm, first = sb("neg_max", [P, NT]), sb("inv_sum", [P, NT]), sb("first_rank", [P, NT])
        cT = sb("combineT", [E, NT, P])
        order = sb("order", [P, E])
        NB = 4
        acc = sb("acc", [P, NB, D])
        or_ok, t_ps, t_sb, l_ps, gt, ex_ok, cb_ok, ct_ps, ct_sb, b_ps, y_ps, a_ok = (
            sem("order_ok"), sem("xT_psum"), sem("xT_sbuf"), sem("logits_psum"), sem("gate_steps"), sem("exps_ok"), sem("combine_ok"),
            sem("combineT_psum"), sem("combineT_sbuf"), sem("bias_psum"), sem("expert_psum"), sem("accumulated"))
        st = g.out_stored
        ln = LayerNorm(nc, ctx, "moeln", g.eps[:, 0:1])
        block = ctx.enter_context(nc.Block())
        NE2 = E // 2
        YB = [3, 4, 5, 6, 7, 2]
        NA = E + 1

        @block.sync
        def _(sp):
            for c in range(NT):
                sp.wait_ge(ln.y_ok, c + 1)
                for b in range(B):
                    sp.dma_start(g.out[b, c * R:(c + 1) * R, :], g.X[R * b:R * b + R, c, :]).then_inc(st, 16)
            sp.wait_ge(st, 16 * B * NT)

        @block.tensor
        def _(pe):
            def experts(c):
                for e2 in range(NE2):
                    n = c * NE2 + e2
                    if n == len(YB) - 1:
                        pe.wait_ge(gt, 1)
                    if n >= len(YB):
                        m, r = (n - len(YB)) // NE2, (n - len(YB)) % NE2
                        pe.wait_ge(a_ok, NA * m + 1 + 2 * (r + 1))
                    for k in range(KD):
                        last = nc.tensor.matmul(ps[:, YB[n % len(YB)], :], xT[:, c, k, :], We[:, k, 2 * e2:2 * e2 + 2, :].rearrange("p e n -> p (e n)"),
                                                start=(k == 0), stop=(k == KD - 1))
                    last.then_inc(y_ps, 1)

            def biases(c):
                if c >= 2:
                    pe.wait_ge(a_ok, NA * (c - 2) + 1)
                nc.tensor.matmul(ps[:, c % 2, 0:D], cT[:, c, :], be[:, :], start=True, stop=True).then_inc(b_ps, 1)

            for c in range(NT):
                if c >= 2:
                    pe.wait_ge(t_sb, c - 1)
                for k in range(KD):
                    last = nc.tensor.transpose(ps[:, c % 2, k * P:(k + 1) * P], g.X[:, c, k * P:(k + 1) * P], g.idf[:, :])
                last.then_inc(t_ps, 1)
            for c in range(NT):
                pe.wait_ge(t_sb, c + 1)
                if c == 0:
                    pe.wait_ge(g.we_ld, 16 * (2 + E))
                for k in range(KD):
                    last = nc.tensor.matmul(ps[:, 2, c * E:(c + 1) * E], xT[:, c, k, :], Wg[:, k, :], start=(k == 0), stop=(k == KD - 1))
            last.then_inc(l_ps, 1)
            experts(0)
            pe.wait_ge(cb_ok, 1)
            for q in range(NG):
                if q >= 2:
                    pe.wait_ge(ct_sb, q - 1)
                for j in range(G4):
                    last = nc.tensor.transpose(ps[0:E, q % 2, j * P:(j + 1) * P], cb[:, q * G4 + j, :], g.idf[:, :])
                last.then_inc(ct_ps, 1)
            pe.wait_ge(ct_sb, NG)
            biases(0)
            for c in range(1, NT):
                biases(c)
                experts(c)

        @block.scalar
        def _(act):
            for c in range(NT):
                act.wait_ge(t_ps, c + 1)
                nc.scalar.copy(xT[:, c, :, :], ps[:, c % 2, 0:KD * P].rearrange("p (k m) -> p k m", k=KD)).then_inc(t_sb, 1)
            act.wait_ge(gt, 3)
            nc.scalar.activation(pr[:, :, :], lg[:, :, :], ACT.Exp).then_inc(ex_ok, 1)
            for q in range(NG):
                act.wait_ge(ct_ps, q + 1)
                nc.scalar.copy(cT[:, q * G4:(q + 1) * G4, :], ps[0:E, q % 2, :].rearrange("p (c m) -> p c m", c=G4)).then_inc(ct_sb, 1)
            for c in range(NT):
                ln.std(act, c)

        @block.gpsimd
        def _(pool):
            for e in range(E):
                nc.gpsimd.memset(order[:, e:e + 1], float(E - e)).then_inc(or_ok, 1)

        @block.vector
        def _(dve):
            per_tile = lambda t: bcast(t[:, :], [[1, NT], [0, E]])
            dve.wait_ge(l_ps, 1)
            nc.vector.tensor_copy(lg[:, :, :], ps[:, 2, 0:NT * E].rearrange("p (c e) -> p c e", c=NT)).then_inc(gt, 1)
            dve.wait_ge(gt, 1)
            nc.vector.tensor_reduce(mxl[:, :], lg[:, :, :], AX.X, ALU.max).then_inc(gt, 1)
            dve.wait_ge(gt, 2)
            nc.vector.tensor_tensor(lg[:, :, :], lg[:, :, :], per_tile(mxl), ALU.subtract).then_inc(gt, 1)
            dve.wait_ge(gt, 3)
            dve.wait_ge(or_ok, E)
            nc.vector.scalar_tensor_tensor(out=rk[:, :, :], in0=lg[:, :, :], scalar=0.0, in1=bcast(order[:, :], [[0, NT], [1, E]]),
                                           op0=ALU.is_equal, op1=ALU.mult).then_inc(gt, 1)
            dve.wait_ge(gt, 4)
            nc.vector.tensor_reduce(first[:, :], rk[:, :, :], AX.X, ALU.max).then_inc(gt, 1)
            dve.wait_ge(gt, 5)
            nc.vector.tensor_tensor(rk[:, :, :], rk[:, :, :], per_tile(first), ALU.is_equal).then_inc(gt, 1)
            dve.wait_ge(ex_ok, 1)
            nc.vector.tensor_reduce(sm[:, :], pr[:, :, :], AX.X, ALU.add).then_inc(gt, 1)
            dve.wait_ge(gt, 7)
            nc.vector.reciprocal(sm[:, :], sm[:, :]).then_inc(gt, 1)
            dve.wait_ge(gt, 8)
            nc.vector.tensor_tensor(cb[:, :, :], rk[:, :, :], per_tile(sm), ALU.mult).then_inc(cb_ok, 1)
            dve.wait_ge(cb_ok, 1)

            def add(c):
                s = c % NB
                dve.wait_ge(b_ps, c + 1)
                if c >= NB:
                    dve.wait_ge(ln.y_ok, c - NB + 1)
                nc.vector.tensor_tensor(acc[:, s, :], g.X[:, c, :], ps[:, c % 2, 0:D], ALU.add).then_inc(a_ok, 1)
                for e in range(E):
                    n = c * NE2 + e // 2
                    if e % 2 == 0:
                        dve.wait_ge(y_ps, n + 1)
                    dve.wait_ge(a_ok, NA * c + e + 1)
                    nc.vector.scalar_tensor_tensor(out=acc[:, s, :], in0=ps[:, YB[n % len(YB)], (e % 2) * D:(e % 2 + 1) * D], scalar=cb[:, c, e:e + 1],
                                                   in1=acc[:, s, :], op0=ALU.mult, op1=ALU.add).then_inc(a_ok, 1)
                dve.wait_ge(a_ok, NA * (c + 1))
                ln.stats(dve, c, acc[:, s, :])

            def normalize(c):
                ln.rstd(dve, c)
                ln.apply(dve, c, g.X[:, c, :], acc[:, c % NB, :])

            for c in range(NT):
                add(c)
                ln.mean_var(dve, c)
                if c:
                    normalize(c - 1)
            normalize(NT - 1)


def program(nc, g, upto=99):
    with ExitStack() as ctx:
        sb = lambda n, s, d=F32: ctx.enter_context(nc.sbuf_tensor(n, s, d))
        g.ps = ctx.enter_context(nc.psum_tensor("psum", [P, 8, 512], F32))
        g.out_stored = ctx.enter_context(nc.semaphore("output_stored"))
        g.X = sb("x_rows", [P, NT, D])
        g.idf, g.idb = sb("identity", [P, P]), sb("identity_bf16", [P, P], BF16)
        g.maskq, g.maskk = sb("mask_q_rows", [P, P], BF16), sb("mask_k_rows", [P, P], BF16)
        g.eps = sb("epsilons", [P, 2])
        rows32k = sb("rows_32k", [P, NT * 2 * D])
        g.QKR = rows32k[:, :].rearrange("p (c n) -> p c n", c=NT)
        g.AT = rows32k[:, :].rearrange("p (c i h) -> p c i h", c=NT, i=R)
        g.VN = rows32k[:, :].rearrange("p (b k n) -> p b k n", b=B, k=4)
        with ExitStack() as c2:
            sb2 = lambda n, s, d=F32: c2.enter_context(nc.sbuf_tensor(n, s, d))
            g.V = sb2("v_rows", [P, NT, D])
            g.KB = sb2("kb_rows", [P, NT, D])
            g.KT = sb2("kT", [P, HG, B, N])
            g.beta = sb2("beta", [P, NT, H])
            phase_qkv(nc, g)
            if upto <= 1:
                return
            g.TT = sb2("invT", [P, NT, R, H])
            phase_delta(nc, g)
            if upto <= 2:
                return
        g.ca, g.cp, g.cpb = sb("c_attn", [P, 3, D]), sb("c_proj", [P, KD, D]), sb("c_proj_b", [P, D])
        g.q_bias, g.k_bias, g.v_bias = sb("q_bias", [P, KD]), sb("k_bias", [HD, 1]), sb("v_bias", [P, HD])
        g.l1_ld, g.ffn_ld, g.phase_ld = (ctx.enter_context(nc.semaphore(n)) for n in ("l1_params_loaded", "ffn_params_loaded", "ffn_phase_loaded"))
        with ExitStack() as c2:
            OT = c2.enter_context(nc.sbuf_tensor("l0_heads_out", [P, HG, NT, P], F32))
            phase_attention(nc, g, "l0", OT, False, g.parts_d, 2 * P, lambda b, kb, h: g.VN[:, b, kb, 32 * h:32 * h + 32])
            sb2 = lambda n, s, d=F32: c2.enter_context(nc.sbuf_tensor(n, s, d))
            Wo = sb2("l0_wo", [P, KD, D])
            g.Wap, g.bap = sb2("w_amp_phase", [P, KD, 2 * D]), sb2("b_amp_phase", [P, 2 * D])
            g.Wst, g.bst = sb2("w_stages", [P, 4, KD, D]), sb2("b_stages", [P, 4, D])
            g.gam, g.bet = sb2("ln_gamma", [P, 4, D]), sb2("ln_beta", [P, 4, D])
            raw_weights = ExitStack()
            alloc_ffn_weights(nc, g, raw_weights)

            def load_wo(sp, s):
                if sp is not None:
                    sp.dma_start(Wo[:, :, :], g.Wo.rearrange("(k p) n -> p k n", p=P)).then_inc(s, 16)
                    load_ffn_weights(sp, g)
                return Wo

            with raw_weights:
                phase_out_proj(nc, g, "l0p", OT, load_wo, None)
                if upto <= 3:
                    return
                phase_weights(nc, g)
            phase_ffn(nc, g)
            if upto <= 4:
                return
        g.We, g.Wg, g.be = sb("expert_w", [P, KD, E, D]), sb("gate_w", [P, KD, E]), sb("expert_b", [E, D])
        g.we_ld = ctx.enter_context(nc.semaphore("expert_weights_loaded"))
        with ExitStack() as c2:
            sb2 = lambda n, s, d=F32: c2.enter_context(nc.sbuf_tensor(n, s, d))
            OT = sb2("l1_heads_out", [P, HG, NT, P])
            g.cpT, g.VA1 = sb2("c_projT", [P, KD, D]), sb2("v1_rows", [P, B * 4, 2 * HD])
            phase_l1_qkv(nc, g)
            phase_attention(nc, g, "l1", OT, True, g.parts_d, 2 * P, lambda b, kb, h: g.VA1[:, 4 * b + kb, :])

            def load_cp(sp, s):
                if sp is not None:
                    sp.sem_inc(s, 16)
                    sp.dma_start(g.Wg[:, :, :], g.d["L1_ffn_Wg"].rearrange("(k p) n -> p k n", p=P)).then_inc(g.we_ld, 16)
                    sp.dma_start(g.be[:, :], g.d["L1_ffn_b"]).then_inc(g.we_ld, 16)
                    for e in range(E):
                        sp.dma_start(g.We[:, :, e, :], g.d["L1_ffn_W"][e].rearrange("(k p) n -> p k n", p=P)).then_inc(g.we_ld, 16)
                return g.cpT

            phase_out_proj(nc, g, "l1p", OT, load_cp, g.cpb)
            if upto <= 5:
                return
        phase_moe(nc, g)


def consts():
    low = np.float32(-3e38)
    q, k = np.arange(P)[:, None], np.arange(P)[None, :]
    inv = (1.0 / (np.float32(10000.0) ** (np.arange(0, HD, 2, dtype=np.float32) / np.float32(HD)))).astype(np.float32)
    th = (np.arange(N, dtype=np.float32)[:, None] * inv).astype(np.float32)
    cos, sin = np.cos(th), np.sin(th)
    lay = lambda a: np.ascontiguousarray(np.tile(a.reshape(NT, R, HD).transpose(1, 0, 2), (B, 1, 1)), dtype=np.float32)
    return {
        "ident": np.eye(P, dtype=np.float32),
        "maskq": np.where(k > q, low, np.float32(0)),
        "maskk": np.where(k < q, low, np.float32(0)),
        "cos": lay(np.concatenate([cos, cos], 1)), "sin": lay(np.concatenate([-sin, sin], 1)),
    }


_INS = ["L0_attn_x", "L0_attn_Wq", "L0_attn_Wk", "L0_attn_Wv", "L0_attn_Wo", "L0_attn_Wb", "L0_ffn_amp_w", "L0_ffn_amp_b",
        "L0_ffn_ph_w", "L0_ffn_ph_b", "L0_ffn_ent_w", "L0_ffn_ent_b", "L0_ffn_ent_pw", "L0_ffn_ent_pb", "L0_ffn_path_w",
        "L0_ffn_path_b", "L0_ffn_phase", "L0_ffn_ln3_g", "L0_ffn_ln3_b", "L0_ffn_ln4_g", "L0_ffn_ln4_b",
        "L1_attn_c_attn_w", "L1_attn_c_attn_b", "L1_attn_c_proj_w", "L1_attn_c_proj_b", "L1_ffn_Wg", "L1_ffn_W", "L1_ffn_b"]


def build(nc, arrays, upto=99):
    g = Ctx()
    d = {n: nc.dram_tensor(f"in_{n}_dram", a.shape, mybir.dt.from_np(a.dtype), kind="ExternalInput").ap() for n, a in arrays.items()}
    g.x_in, g.Wq, g.Wk, g.Wv, g.Wo, g.Wb = (d[n] for n in _INS[:6])
    g.d = d
    g.ident_d, g.maskq_d, g.maskk_d, g.cos_d, g.sin_d = (d[n] for n in ("ident", "maskq", "maskk", "cos", "sin"))
    g.out = nc.dram_tensor("out_0_dram", (B, N, D), F32, kind="ExternalOutput").ap()
    scratch = lambda n, s, t: nc.dram_tensor(n, s, t, kind="Internal").ap()
    g.parts_d = scratch("parts_scratch", (NPART, 4, P, B * N), BF16)
    g.gram_d = scratch("gram_scratch", (P, NT * 2 * H * CH), F32)
    g.inv_d = scratch("inverse_scratch", (2, P, CH * H * CH), F32)
    program(nc, g, upto)


def kernel(**inputs):
    import concourse.bacc as _bacc
    from concourse.bass_utils import run_bass_kernel_spmd as _run

    nc = _bacc.Bacc("TRN2", target_bir_lowering=False, num_devices=1)
    arrays = {n: np.ascontiguousarray(inputs[n]) for n in _INS}
    arrays.update(consts())
    build(nc, arrays)
    r = _run(nc, [{f"in_{n}_dram": a for n, a in arrays.items()}], core_ids=[0])
    return r.results[0]["out_0_dram"]
```
